# Optimizing a Trainium2 kernel written in Bass

```python
import numpy as np
import jax
import jax.numpy as jnp

def _softmax(x, axis=-1):
    return jax.nn.softmax(x, axis=axis)

def _gelu(x):
    return jax.nn.gelu(x, approximate=True)

def _silu(x):
    return jax.nn.silu(x)

def _sigmoid(x):
    return jax.nn.sigmoid(x)

def _layernorm(x, axis=-1, eps=1e-05):
    m = jnp.mean(x, axis=axis, keepdims=True)
    v = jnp.var(x, axis=axis, keepdims=True)
    return (x - m) / jnp.sqrt(v + eps)

def _scatter_add(tgt, idx, src, axis=0):
    return tgt.at[idx].add(src)

def _segment_sum(src, seg, n):
    return jax.ops.segment_sum(src, seg, n)
kernel_name = 'mk_seq_postln_d1_jaxref_r4_5118e9'

def setup_inputs(seed: int=0):
    np.random.seed(seed)
    _w = jnp.asarray

    def _L0_attn_setup():
        import jax, jax.numpy as jnp
        import numpy as np
        D_IN = 512
        D_OUT = 512
        NUM_HEADS = 16
        NUM_KV_GROUPS = 4
        GROUP_SIZE = NUM_HEADS // NUM_KV_GROUPS
        HEAD_DIM = D_OUT // NUM_HEADS
        key = jax.random.key(seed)
        ks = jax.random.split(key, 6)
        b, n = (2, 512)
        x = jax.random.normal(ks[0], (b, n, D_IN), dtype=jnp.float32)
        Wq = jax.random.normal(ks[1], (D_IN, D_OUT), dtype=jnp.float32) * (1.0 / np.sqrt(D_IN))
        Wk = jax.random.normal(ks[2], (D_IN, NUM_KV_GROUPS * HEAD_DIM), dtype=jnp.float32) * (1.0 / np.sqrt(D_IN))
        Wv = jax.random.normal(ks[3], (D_IN, NUM_KV_GROUPS * HEAD_DIM), dtype=jnp.float32) * (1.0 / np.sqrt(D_IN))
        Wo = jax.random.normal(ks[4], (D_OUT, D_OUT), dtype=jnp.float32) * (1.0 / np.sqrt(D_OUT))
        bo = jax.random.normal(ks[5], (D_OUT,), dtype=jnp.float32) * 0.01
        return {'x': x, 'Wq': Wq, 'Wk': Wk, 'Wv': Wv, 'Wo': Wo, 'bo': bo}
    _L0_attn_in = _L0_attn_setup()

    def _L0_ffn_setup():
        import jax, jax.numpy as jnp
        import numpy as np
        LN_EPS = 1e-05
        L2_EPS = 1e-12

        def _l2norm(v, axis):
            n = jnp.sqrt(jnp.sum(v * v, axis=axis, keepdims=True))
            return v / jnp.maximum(n, L2_EPS)
        key = jax.random.key(seed)
        ks = jax.random.split(key, 4)
        B, N, D, E, S, H = (8, 512, 512, 16, 128, 128)
        x = jax.random.normal(ks[0], (B, N, D), dtype=jnp.float32)
        mu = jax.random.normal(ks[1], (D, E, S), dtype=jnp.float32) / np.sqrt(D)
        W1 = jax.random.normal(ks[2], (E, D, H), dtype=jnp.float32) * np.sqrt(2.0 / D)
        W2 = jax.random.normal(ks[3], (E, H, D), dtype=jnp.float32) * np.sqrt(2.0 / (H + D))
        return {'x': x, 'gamma': jnp.ones((D,), jnp.float32), 'beta': jnp.zeros((D,), jnp.float32), 'mu': mu, 'scale': jnp.ones((1,), jnp.float32), 'W1': W1, 'b1': jnp.zeros((E, H), jnp.float32), 'W2': W2, 'b2': jnp.zeros((E, D), jnp.float32)}
    _L0_ffn_in = _L0_ffn_setup()
    _d = {'L0_attn_x': _L0_attn_in['x'], 'L0_attn_Wq': _L0_attn_in['Wq'], 'L0_attn_Wk': _L0_attn_in['Wk'], 'L0_attn_Wv': _L0_attn_in['Wv'], 'L0_attn_Wo': _L0_attn_in['Wo'], 'L0_attn_bo': _L0_attn_in['bo'], 'L0_ffn_gamma': _L0_ffn_in['gamma'], 'L0_ffn_beta': _L0_ffn_in['beta'], 'L0_ffn_mu': _L0_ffn_in['mu'], 'L0_ffn_scale': _L0_ffn_in['scale'], 'L0_ffn_W1': _L0_ffn_in['W1'], 'L0_ffn_b1': _L0_ffn_in['b1'], 'L0_ffn_W2': _L0_ffn_in['W2'], 'L0_ffn_b2': _L0_ffn_in['b2']}
    _x0 = _d['L0_attn_x']
    _d['L0_attn_x'] = jax.random.normal(jax.random.fold_in(jax.random.key(seed), 1), (2, 2048, 512), dtype=_x0.dtype)
    del _x0
    return _d

def reference(L0_attn_x, L0_attn_Wq, L0_attn_Wk, L0_attn_Wv, L0_attn_Wo, L0_attn_bo, L0_ffn_gamma, L0_ffn_beta, L0_ffn_mu, L0_ffn_scale, L0_ffn_W1, L0_ffn_b1, L0_ffn_W2, L0_ffn_b2):

    def _L0_attn_ref(x, Wq, Wk, Wv, Wo, bo):
        import jax, jax.numpy as jnp
        import numpy as np
        D_IN = 512
        D_OUT = 512
        NUM_HEADS = 16
        NUM_KV_GROUPS = 4
        GROUP_SIZE = NUM_HEADS // NUM_KV_GROUPS
        HEAD_DIM = D_OUT // NUM_HEADS
        b, n, _ = x.shape
        q = (x @ Wq).reshape(b, n, NUM_KV_GROUPS, GROUP_SIZE, HEAD_DIM)
        k = (x @ Wk).reshape(b, n, NUM_KV_GROUPS, HEAD_DIM)
        v = (x @ Wv).reshape(b, n, NUM_KV_GROUPS, HEAD_DIM)
        scale = 1.0 / np.sqrt(HEAD_DIM).astype(np.float32)
        scores = jnp.einsum('bqgsd,bkgd->bgsqk', q, k) * scale
        causal = jnp.arange(n)[:, None] < jnp.arange(n)[None, :]
        scores = jnp.where(causal, -jnp.inf, scores)
        attn = jax.nn.softmax(scores, axis=-1)
        ctx = jnp.einsum('bgsqk,bkgd->bqgsd', attn, v)
        ctx = ctx.reshape(b, n, D_OUT)
        return ctx @ Wo + bo

    def _L0_ffn_ref(x, gamma, beta, mu, scale, W1, b1, W2, b2):
        import jax, jax.numpy as jnp
        import numpy as np
        LN_EPS = 1e-05
        L2_EPS = 1e-12

        def _l2norm(v, axis):
            n = jnp.sqrt(jnp.sum(v * v, axis=axis, keepdims=True))
            return v / jnp.maximum(n, L2_EPS)
        B, N, D = x.shape
        _, E, S = mu.shape
        mean = jnp.mean(x, axis=-1, keepdims=True)
        var = jnp.mean(jnp.square(x - mean), axis=-1, keepdims=True)
        x_ln = (x - mean) / jnp.sqrt(var + LN_EPS) * gamma + beta
        x_n = _l2norm(x_ln, -1) * scale
        mu_n = _l2norm(mu, 0)
        logits = jnp.einsum('bnd,des->bnes', x_n, mu_n)
        dispatch = jax.nn.softmax(logits, axis=1)
        combine = jax.nn.softmax(logits.reshape(B, N, E * S), axis=-1)
        slot_in = jnp.einsum('bnd,bnes->besd', x_ln, dispatch)
        h = jax.nn.gelu(jnp.einsum('besd,edh->besh', slot_in, W1) + b1[None, :, None, :], approximate=False)
        slot_out = jnp.einsum('besh,ehd->besd', h, W2) + b2[None, :, None, :]
        out = jnp.einsum('bsd,bns->bnd', slot_out.reshape(B, E * S, D), combine)
        return out
    x = L0_attn_x
    x = _layernorm(x + _L0_attn_ref(x, L0_attn_Wq, L0_attn_Wk, L0_attn_Wv, L0_attn_Wo, L0_attn_bo), axis=-1)
    x = _layernorm(x + _L0_ffn_ref(x, L0_ffn_gamma, L0_ffn_beta, L0_ffn_mu, L0_ffn_scale, L0_ffn_W1, L0_ffn_b1, L0_ffn_W2, L0_ffn_b2), axis=-1)
    return x

_drawn_inputs = setup_inputs


def setup_inputs(seed=0):
    import zlib

    import numpy as np

    out = dict(_drawn_inputs(seed))
    spreads = {'L0_ffn_gamma': (1.0, 0.6),
     'L0_ffn_beta': (0.0, 0.781),
     'L0_ffn_b1': (0.0, 0.8),
     'L0_ffn_b2': (0.0, 0.333)}
    factors = {'L0_attn_bo': 5.478, 'L0_ffn_mu': 8.0, 'L0_ffn_W1': 4.821, 'L0_ffn_W2': 4.066}
    for name, (base, spread) in spreads.items():
        noise = np.random.default_rng([zlib.crc32(name.encode()), seed]).standard_normal(out[name].shape)
        drawn = base * np.exp(spread * noise) if base else spread * noise
        out[name] = jnp.asarray(drawn.astype(out[name].dtype))
    for name, factor in factors.items():
        out[name] = (out[name] * factor).astype(out[name].dtype)
    return out
```

```python
import concourse.bass as bass
from concourse import mybir
from contextlib import ExitStack
import numpy as np

F32 = mybir.dt.float32
F32R = mybir.dt.float32r
BF16 = mybir.dt.bfloat16
ALU = mybir.AluOpType
ACT = mybir.ActivationFunctionType
AX = mybir.AxisListType

P = 128
BANK = 512
B, N, D = 2, 2048, 512
HEADS, GROUPS, HD = 16, 4, 32
HPG = HEADS // GROUPS
E, S, H = 16, 128, 128
DC = D // P
TOK = B * N
BLK = 512
NBLK = TOK // BLK
NT = N // P
QB = N // BLK
ITERS = B * GROUPS
SCALE = float(np.float32(1.0) / np.sqrt(np.float32(HD)))
MASKED = -1.0e38
LN_EPS = 1e-5
L2_EPS = 1e-12
QKV = HEADS * HD + 2 * GROUPS * HD
QROWS = 3 * HD
MROWS = QROWS + 2


class Names:

    def __init__(self, nc, ctx, sems):
        self.nc, self.ctx, self.sems = nc, ctx, sems

    def sbuf(self, name, shape, dt=F32):
        return self.ctx.enter_context(self.nc.sbuf_tensor(name, shape, dt))

    def psum(self, name, banks):
        return self.ctx.enter_context(self.nc.psum_tensor(name, [P, banks, BANK], F32))

    def sem(self, name):
        handle = self.nc.alloc_semaphore(name=name)
        self.sems.append(handle)
        return handle


def three_passes(pe, out, w_hi, w_lo, m_hi, m_lo, start, stop):
    pe.matmul(out, w_hi, m_hi, start=start, stop=False)
    pe.matmul(out, w_hi, m_lo, start=False, stop=False)
    return pe.matmul(out, w_lo, m_hi, start=False, stop=stop)


def projections(nc, sems, x, Wq, Wk, Wv, d):
    with ExitStack() as ctx:
        al = Names(nc, ctx, sems)
        ident = al.sbuf("p1_ident", [P, P])
        w_raw = al.sbuf("p1_w", [P, DC, QKV])
        w_hi = al.sbuf("p1_w_hi", [P, DC, QKV], F32R)
        w_lo = al.sbuf("p1_w_lo", [P, DC, QKV], F32R)
        x_in = [al.sbuf(f"p1_x{j}", [P, 4, D]) for j in range(2)]
        xT_hi = [al.sbuf(f"p1_xT_hi{j}", [P, DC, BLK], F32R) for j in range(2)]
        xT_lo = [al.sbuf(f"p1_xT_lo{j}", [P, DC, BLK], F32R) for j in range(2)]
        NF = GROUPS + 1
        f_hi = al.sbuf("p1_f_hi", [P, NF, BLK], F32R)
        f_lo = al.sbuf("p1_f_lo", [P, NF, BLK], F32R)
        FB, F0 = NF + 1, 4
        v_out = [al.sbuf(f"p1_v{j}", [P, 4, P]) for j in range(2)]
        ps_t = al.psum("p1_ps_t", DC)
        ps_f = al.psum("p1_ps_f", 4)

        s_ident0, s_ident = al.sem("p1_ident0"), al.sem("p1_ident")
        s_w, s_whi, s_wlo = al.sem("p1_w"), al.sem("p1_whi"), al.sem("p1_wlo")
        s_x = [al.sem(f"p1_x_loaded{j}") for j in range(2)]
        s_xt, s_xhi, s_xlo = al.sem("p1_transposed"), al.sem("p1_x_hi"), al.sem("p1_x_lo")
        s_f, s_fhi, s_flo = al.sem("p1_features"), al.sem("p1_f_hi"), al.sem("p1_f_lo_and_v")
        s_ohi = [al.sem(f"p1_stored_hi{m}") for m in range(NF)]
        s_olo = [al.sem(f"p1_stored_lo{m}") for m in range(NF)]
        s_ov = [al.sem(f"p1_stored_v{j}") for j in range(2)]

        block = ctx.enter_context(nc.Block())
        x_b = x.rearrange("b n c -> (b n) c")

        @block.sync
        def _(sp):
            for w, a, z in ((Wq, 0, D), (Wk, D, D + P), (Wv, D + P, QKV)):
                sp.dma_start(w_raw[:, :, a:z], w.rearrange("(c p) n -> p c n", p=P)).then_inc(s_w, 16)

            def load(blk, j):
                sp.dma_start(x_in[j][:, :, :], x_b[bass.ds(blk * BLK, BLK), :]
                             .rearrange("(t p) c -> p t c", p=P)).then_inc(s_x[j], 16)

            def store(blk, j):
                b, cols = blk // QB, bass.ds(blk % QB * BLK, BLK)
                for m in range(NF):
                    for half, src, done in ((0, f_hi, s_ohi), (1, f_lo, s_olo)):
                        if half == 0:
                            sp.wait_ge(s_fhi, blk * NF + (m + 1))
                        else:
                            sp.wait_ge(s_flo, blk * FB + (F0 + m + 1))
                        to = d["q"][b, m, half, :, cols] if m < GROUPS else d["k"][b, half, :, cols]
                        sp.dma_start(to, src[:, m, :].bitcast(F32)).then_inc(done[m], 16)
                sp.wait_ge(s_flo, blk * FB + (F0 + FB))
                sp.dma_start(d["v"][bass.ds(blk * BLK, BLK), :].rearrange("(t p) n -> p t n", p=P), v_out[j][:, :, :]).then_inc(s_ov[j], 16)

            for j in range(2):
                load(j, j)
            with sp.Fori(0, NBLK // 2 - 1) as i:
                at = i * 2
                for j in range(2):
                    store(at + j, j)
                    load(at + (j + 2), j)
            for j in range(2):
                store(NBLK - 2 + j, j)
            for m in range(NF):
                sp.wait_ge(s_ohi[m], 16 + 16 * NBLK)
                sp.wait_ge(s_olo[m], 16 + 16 * NBLK)
            for j in range(2):
                sp.wait_ge(s_ov[j], 16 + 16 * NBLK // 2)

        @block.gpsimd
        def _(pool):
            pool.memset(ident[:, :], 0.0).then_inc(s_ident0, 1)
            pool.wait_ge(s_ident0, 1)
            pool.affine_select(out=ident[:, :], in_=ident[:, :], compare_op=ALU.not_equal, fill=1.0,
                               base=0, pattern=[[-1, P]], channel_multiplier=1).then_inc(s_ident, 1)

        @block.tensor
        def _(pe):
            pe.wait_ge(s_ident, 1)
            pe.wait_ge(s_whi, 1)
            pe.wait_ge(s_wlo, 1)

            def transposes(blk, j, n):
                pe.wait_ge(s_x[j], n * 16 + 16)
                for c in range(DC):
                    pe.wait_ge(s_xlo, blk * DC + (c + 1))
                    for t in range(4):
                        last = pe.transpose(ps_t[:, c, t * P:(t + 1) * P], x_in[j][:, t, c * P:(c + 1) * P], ident[:, :])
                    last.then_inc(s_xt, 1)

            def features(blk, j, ms):
                for m in ms:
                    bank = (FB * j + m) % 4
                    if m == 0:
                        pe.wait_ge(s_xlo, blk * DC + 2 * DC)
                    pe.wait_ge(s_flo, blk * FB + (m + 1))
                    if m < NF:
                        for c in range(DC):
                            w = bass.ts(m, P)
                            last = three_passes(pe, ps_f[:, bank, :], w_hi[:, c, w], w_lo[:, c, w],
                                                xT_hi[j][:, c, :], xT_lo[j][:, c, :], c == 0, c == DC - 1)
                    else:
                        for t in range(4):
                            for c in range(DC):
                                w, n = bass.ts(m, P), bass.ts(t, P)
                                last = three_passes(pe, ps_f[:, bank, n], xT_hi[j][:, c, n], xT_lo[j][:, c, n],
                                                    w_hi[:, c, w], w_lo[:, c, w], c == 0, c == DC - 1)
                    last.then_inc(s_f, 1)

            def pair(at, half, ends):
                features(at, 0, range(0, 2))
                transposes(at + 1, 1, half)
                features(at, 0, range(2, FB))
                features(at + 1, 1, range(0, 2))
                if not ends:
                    transposes(at + 2, 0, half + 1)
                features(at + 1, 1, range(2, FB))

            transposes(0, 0, 0)
            with pe.Fori(0, NBLK // 2 - 1) as i:
                pair(i * 2, i, False)
            pair(NBLK - 2, NBLK // 2 - 1, True)

        @block.scalar
        def _(act):
            def split_hi(blk, j):
                act.wait_ge(s_f, blk * FB + FB)
                for c in range(DC):
                    act.wait_ge(s_xt, blk * DC + (c + 1))
                    act.activation(xT_hi[j][:, c, :], ps_t[:, c, :], ACT.Copy).then_inc(s_xhi, 1)

            def features_hi(blk, j, ms):
                for m in ms:
                    act.wait_ge(s_f, blk * FB + (2 * FB + m + 1))
                    act.wait_ge(s_ohi[m], blk * 16 + 16)
                    act.activation(f_hi[:, m, :], ps_f[:, (FB * j + m) % 4, :], ACT.Copy,
                                   scale=SCALE if m < GROUPS else 1.0).then_inc(s_fhi, 1)

            def pair(at, ends):
                features_hi(at, 0, range(0, 2))
                split_hi(at + 1, 1)
                features_hi(at, 0, range(2, NF))
                features_hi(at + 1, 1, range(0, 2))
                if not ends:
                    split_hi(at + 2, 0)
                features_hi(at + 1, 1, range(2, NF))

            split_hi(0, 0)
            with act.Fori(0, NBLK // 2 - 1) as i:
                pair(i * 2, False)
            pair(NBLK - 2, True)

        @block.vector
        def _(dve):
            dve.sem_inc(s_xlo, DC)
            dve.sem_inc(s_flo, F0)
            dve.sem_inc(s_f, 2 * FB)
            for done in s_ohi + s_olo + s_ov:
                dve.sem_inc(done, 16)
            dve.wait_ge(s_w, 48)
            dve.tensor_copy(w_hi[:, :, :], w_raw[:, :, :]).then_inc(s_whi, 1)
            dve.wait_ge(s_whi, 1)
            dve.tensor_tensor(w_lo[:, :, :], w_raw[:, :, :], w_hi[:, :, :], ALU.subtract).then_inc(s_wlo, 1)

            def split_lo(blk, j):
                for c in range(DC):
                    dve.wait_ge(s_xhi, blk * DC + (c + 1))
                    dve.tensor_tensor(xT_lo[j][:, c, :], ps_t[:, c, :], xT_hi[j][:, c, :], ALU.subtract).then_inc(s_xlo, 1)

            def features_lo(blk, j, ms):
                for m in ms:
                    dve.wait_ge(s_fhi, blk * NF + (m + 1))
                    dve.wait_ge(s_olo[m], blk * 16 + 16)
                    dve.scalar_tensor_tensor(out=f_lo[:, m, :], in0=ps_f[:, (FB * j + m) % 4, :],
                                             scalar=SCALE if m < GROUPS else 1.0, in1=f_hi[:, m, :],
                                             op0=ALU.mult, op1=ALU.subtract).then_inc(s_flo, 1)

            def values(blk, j, half):
                dve.wait_ge(s_f, blk * FB + 3 * FB)
                dve.wait_ge(s_ov[j], half * 16 + 16)
                dve.tensor_copy(v_out[j][:, :, :], ps_f[:, (FB * j + NF) % 4, :]).then_inc(s_flo, 1)

            def pair(at, half, ends):
                features_lo(at, 0, range(0, 2))
                split_lo(at + 1, 1)
                features_lo(at, 0, range(2, NF))
                values(at, 0, half)
                features_lo(at + 1, 1, range(0, 2))
                if not ends:
                    split_lo(at + 2, 0)
                features_lo(at + 1, 1, range(2, NF))
                values(at + 1, 1, half)

            split_lo(0, 0)
            with dve.Fori(0, NBLK // 2 - 1) as i:
                pair(i * 2, i, False)
            pair(NBLK - 2, NBLK // 2 - 1, True)


LAG = 2
RING = 4
M_BANKS, ST_BANKS = 4, 2
STEPS = [(qb, kt) for qb in range(QB) for kt in range(4 * (qb + 1))]
NS = len(STEPS)
ENDS = [4 * (qb + 1) * (qb + 2) // 2 for qb in range(QB)]
UNITS = [(qt, h, c) for qt in range(NT) for h in range(HPG) for c in range(qt // 4 + 1)]
NU = len(UNITS)
M_FROM, M_TO = 4, 36
ADDED = [[kt for kt in range(4 * qb) if kt % 3 != 0] for qb in range(QB)]
ADDS = [max(len(a) - 1, 0) for a in ADDED]
NADD = sum(ADDS)


def adds_before(qb, kt):
    return sum(ADDS[:qb]) + max(ADDED[qb].index(kt), 1)


def order(maxima):
    work, u = [], 0
    per = -(-NU // (M_TO - M_FROM))
    ends = {e - 1: qb for qb, e in enumerate(ENDS)}
    for s in range(NS + LAG + 5):
        for h in range(HPG):
            if s < NS:
                work.append(("scores", s, h))
            if h == 1 and LAG <= s < NS + LAG:
                work.append(("context", s - LAG, None))
                if s - LAG in ends:
                    work.append(("sums", ends[s - LAG], None))
            if maxima and M_FROM <= s < M_TO:
                for _ in range(per // HPG + (h < per % HPG)):
                    if u < NU:
                        work.append(("maximum", u, None))
                        u += 1
        if maxima and s == M_TO:
            work.append(("rows", None, None))
        if s - LAG in ends:
            work.append(("take", ends[s - LAG], None))
            work.append(("normalise", ends[s - LAG], None))
        if s - LAG - 4 in ends:
            work.append(("store", ends[s - LAG - 4], None))
    return work


def attention(nc, sems, d):
    with ExitStack() as ctx:
        al = Names(nc, ctx, sems)
        ident = al.sbuf("p2_ident", [P, P])
        ident_b = al.sbuf("p2_ident_b", [P, P], BF16)
        mask_kq = al.sbuf("p2_mask_kq", [P, P], BF16)
        mask_qk = al.sbuf("p2_mask_qk", [P, P], BF16)
        ones = al.sbuf("p2_ones", [P, HD])
        q_m = al.sbuf("p2_q_m", [QROWS, QB, HPG, BLK], F32R)
        k_m = al.sbuf("p2_k_m", [QROWS, N], F32R)
        q_e = al.sbuf("p2_q_e", [MROWS, QB, HPG, BLK], F32R)
        k_e = al.sbuf("p2_k_e", [MROWS, N], F32R)
        v_e = al.sbuf("p2_v", [P, NT, HD])
        parts = al.sbuf("p2_parts", [P, QB * HPG * 4, QB])
        neg_max = al.sbuf("p2_neg_max", [P, P])
        rows_hi = al.sbuf("p2_rows_hi", [QB * HPG * 4, P], F32R)
        rows_lo = al.sbuf("p2_rows_lo", [QB * HPG * 4, P], F32R)
        probs = [al.sbuf(f"p2_probs{r}", [P, HPG, BLK]) for r in range(RING)]
        added = [al.sbuf(f"p2_added{r}", [P, HPG, BLK]) for r in range(2)]
        raw = [al.sbuf(f"p2_raw{r}", [P, BLK]) for r in range(2)]
        sums = [al.sbuf(f"p2_sums{r}", [P, BLK]) for r in range(2)]
        inv = al.sbuf("p2_inv", [P, BLK])
        out = al.sbuf("p2_out", [P, BLK])
        out_hi = [al.sbuf(f"p2_out_hi{r}", [P, BLK], F32R) for r in range(2)]
        out_lo = [al.sbuf(f"p2_out_lo{r}", [P, BLK], F32R) for r in range(2)]
        ps_s = al.psum("p2_ps_s", ST_BANKS)
        ps_m = al.psum("p2_ps_m", M_BANKS)
        ps_c = al.psum("p2_ps_c", 1)
        ps_d = al.psum("p2_ps_d", 1)

        sem = lambda name: al.sem("p2_" + name)
        s_const, s_const0, s_one = sem("const"), sem("const0"), sem("one")
        s_qm, s_km = [sem(f"q_m{c}") for c in range(QB)], [sem(f"k_m{c}") for c in range(QB)]
        s_qe, s_ke = [sem(f"q_e{c}") for c in range(QB)], [sem(f"k_e{c}") for c in range(QB)]
        s_ve, s_row = [sem(f"v{c}") for c in range(QB)], [sem(f"rows{c}") for c in range(QB)]
        s_unit = sem("unit_scored")
        s_taken = sem("unit_taken")
        s_neg, s_rt = sem("neg_max"), sem("rows_transposed")
        s_rhi, s_rlo = sem("rows_hi"), sem("rows_lo")
        s_score = sem("scored")
        s_exp = sem("exp")
        s_ctx = sem("context")
        s_add = sem("added")
        s_sum = sem("summed")
        s_take = sem("raw_taken")
        s_inv, s_norm, s_hi, s_lo = sem("inverse"), sem("normalised"), sem("ctx_hi"), sem("ctx_lo")
        s_st = [sem(f"ctx_stored{r}") for r in range(2)]

        block = ctx.enter_context(nc.Block())
        UF = NU + 1

        @block.sync
        def _(sp):
            def stacks(qs, ks, s_q, s_k, b, g, c, what):
                n = bass.ts(c, BLK)
                for r in range(3):
                    rows = slice(r * HD, (r + 1) * HD)
                    if "k" in what:
                        sp.dma_start(ks[rows, n].bitcast(F32), d["k"][b, int(r == 2), bass.ds(g * HD, HD), n]).then_inc(s_k[c], 16)
                for r in range(3):
                    rows = slice(r * HD, (r + 1) * HD)
                    if "q" in what:
                        sp.dma_start(qs[rows, c, :, :].bitcast(F32), d["q"][b, g, int(r == 1), :, n]
                                     .rearrange("(h p) n -> p h n", p=HD)).then_inc(s_q[c], 16)

            def for_maxima(b, g):
                for c in range(QB):
                    stacks(q_m, k_m, s_qm, s_km, b, g, c, "kq")

            def rows(c):
                part = slice(c * 4 * HPG, (c + 1) * 4 * HPG)
                for r, src in ((QROWS, rows_hi), (QROWS + 1, rows_lo)):
                    sp.dma_start(q_e[r:r + 1, c, :, :].bitcast(F32), src[part, :].bitcast(F32)).then_inc(s_row[c], 16)

            def iteration(it, b, g, nb, ng):
                for c in range(QB - 1):
                    sp.wait_ge(s_score, it * NS * HPG + ENDS[c] * HPG)
                    stacks(q_e, k_e, s_qe, s_ke, b, g, c, "q")

                def keys(c):
                    sp.wait_ge(s_score, it * NS * HPG + (ENDS[2] + 4 * (c + 1)) * HPG)
                    stacks(q_e, k_e, s_qe, s_ke, b, g, c, "k")
                    sp.wait_ge(s_ctx, it * NS + (ENDS[2] + 4 * (c + 1)))
                    sp.dma_start(v_e[:, 4 * c:4 * c + 4, :], d["v"][bass.ds(b * N + c * BLK, BLK), bass.ds(g * HD, HD)]
                                 .rearrange("(t p) n -> p t n", p=P)).then_inc(s_ve[c], 16)

                keys(0)
                keys(1)
                sp.wait_ge(s_unit, it * NU + NU)
                if nb is not None:
                    for_maxima(nb, ng)
                sp.wait_ge(s_rhi, it + 1)
                sp.wait_ge(s_rlo, it + 1)
                for c in range(QB - 1):
                    rows(c)
                keys(2)
                keys(3)
                stacks(q_e, k_e, s_qe, s_ke, b, g, QB - 1, "q")
                rows(QB - 1)

            for_maxima(0, 0)
            with sp.Fori(0, ITERS - 1) as it:
                iteration(it, it // GROUPS, it % GROUPS, (it + 1) // GROUPS, (it + 1) % GROUPS)
            iteration(ITERS - 1, B - 1, GROUPS - 1, None, None)

        @block.gpsimd
        def _(pool):
            pool.memset(ident[:, :], 0.0).then_inc(s_const0, 1)
            pool.memset(ident_b[:, :], 0.0).then_inc(s_const0, 1)
            pool.memset(mask_kq[:, :], 0.0).then_inc(s_const0, 1)
            pool.memset(mask_qk[:, :], 0.0).then_inc(s_const0, 1)
            pool.memset(ones[:, :], 1.0).then_inc(s_const, 1)
            pool.wait_ge(s_const0, 4)
            for m in (ident, ident_b):
                pool.affine_select(out=m[:, :], in_=m[:, :], compare_op=ALU.not_equal, fill=1.0,
                                   base=0, pattern=[[-1, P]], channel_multiplier=1).then_inc(s_const, 1)
            pool.affine_select(out=mask_kq[:, :], in_=mask_kq[:, :], compare_op=ALU.is_ge, fill=MASKED,
                               base=0, pattern=[[1, P]], channel_multiplier=-1).then_inc(s_const, 1)
            pool.affine_select(out=mask_qk[:, :], in_=mask_qk[:, :], compare_op=ALU.is_ge, fill=MASKED,
                               base=0, pattern=[[-1, P]], channel_multiplier=1).then_inc(s_const, 1)
            pool.sem_inc(s_sum, 2)
            with pool.Fori(0, ITERS) as it:
                for qb in range(1, QB):
                    a = added[qb % 2]
                    pool.wait_ge(s_sum, it * (QB - 1) + {1: 2, 2: 1, 3: 3}[qb])
                    for n, kt in enumerate(ADDED[qb]):
                        if n == 0:
                            continue
                        done = (ENDS[qb - 1] + kt + 1) * HPG
                        pool.wait_ge(s_exp, it * NS * HPG + (ST_BANKS + done))
                        if n > 1:
                            pool.wait_ge(s_add, it * NADD + (adds_before(qb, kt) - 1))
                        first = probs[(ENDS[qb - 1] + ADDED[qb][0]) % RING] if n == 1 else a
                        pool.tensor_tensor(a[:, :, :], first[:, :, :], probs[(ENDS[qb - 1] + kt) % RING][:, :, :],
                                           ALU.add).then_inc(s_add, 1)

        @block.tensor
        def _(pe):
            def unit(it, u):
                qt, h, c = UNITS[u]
                bank, w = ps_m[:, u % M_BANKS, :], min(BLK, (qt + 1) * P - c * BLK)
                if h == 0 and c == 0 and qt % 4 == 0:
                    pe.wait_ge(s_qm[qt // 4], it * 48 + 48)
                    pe.wait_ge(s_km[qt // 4], it * 48 + 48)
                pe.wait_ge(s_taken, it * UF + max(u + 1, M_BANKS))
                last_c = c == qt // 4
                mm = pe.matmul(bank[:, 0:w], q_m[:, qt // 4, h, bass.ts(qt % 4, P)], k_m[:, c * BLK:c * BLK + w],
                               start=True, stop=not last_c)
                if last_c:
                    mm = pe.matmul(bank[:, w - P:w], ident_b[:, :], mask_qk[:, :], start=False, stop=True)
                mm.then_inc(s_unit, 1)

            def rows(it):
                pe.wait_ge(s_neg, it + 1)
                pe.transpose(ps_m[:, 0, 0:P], neg_max[:, :], ident[:, :]).then_inc(s_rt, 1)

            def scores(it, s, h):
                qb, kt = STEPS[s]
                q0 = max(0, kt * P - qb * BLK)
                diagonal = kt >= 4 * qb
                if h == 0 and kt == 0:
                    pe.wait_ge(s_qe[qb], it * 48 + 48)
                    pe.wait_ge(s_row[qb], it * 32 + 64)
                if h == 0 and diagonal and kt % 4 == 0:
                    pe.wait_ge(s_ke[qb], it * 48 + 48)
                pe.wait_ge(s_exp, it * NS * HPG + (s * HPG + h + 1))
                bank = ps_s[:, (s * HPG + h) % ST_BANKS, :]
                mm = pe.matmul(bank[:, q0:BLK], k_e[:, bass.ts(kt, P)], q_e[:, qb, h, q0:BLK],
                               start=True, stop=not diagonal)
                if diagonal:
                    mm = pe.matmul(bank[:, q0:q0 + P], ident_b[:, :], mask_kq[:, :], start=False, stop=True)
                mm.then_inc(s_score, 1)

            def context(it, s):
                qb, kt = STEPS[s]
                q0 = max(0, kt * P - qb * BLK)
                direct, last = kt not in ADDED[qb], kt == 4 * qb + 3
                pe.wait_ge(s_exp, it * NS * HPG + (ST_BANKS + (s + 1) * HPG))
                if kt == 0:
                    pe.wait_ge(s_take, it * 2 * QB + 2 * (qb + 1))
                if kt == 4 * qb:
                    pe.wait_ge(s_ve[qb], it * 16 + 16)
                for h in range(HPG):
                    rows = slice(h * HD, (h + 1) * HD)
                    mm = pe.matmul(ps_c[rows, 0, q0:BLK], v_e[:, kt, :], probs[s % RING][:, h, q0:BLK],
                                   start=kt == 0, stop=last)
                if direct:
                    for h in range(HPG):
                        rows = slice(h * HD, (h + 1) * HD)
                        mm = pe.matmul(ps_d[rows, 0, q0:BLK], ones[:, :], probs[s % RING][:, h, q0:BLK],
                                       start=kt == 0, stop=last and not ADDS[qb])
                mm.then_inc(s_ctx, 1)

            def block_sums(it, qb):
                if ADDS[qb]:
                    pe.wait_ge(s_add, it * NADD + sum(ADDS[:qb + 1]))
                    for h in range(HPG):
                        rows = slice(h * HD, (h + 1) * HD)
                        mm = pe.matmul(ps_d[rows, 0, :], ones[:, :], added[qb % 2][:, h, :], start=False, stop=True)
                    mm.then_inc(s_sum, 1)

            def walk(it, maxima):
                for what, a, h in order(maxima):
                    if what == "maximum":
                        unit(it + 1, a)
                    elif what == "rows":
                        rows(it + 1)
                    elif it is None:
                        continue
                    elif what == "scores":
                        scores(it, a, h)
                    elif what == "context":
                        context(it, a)
                    elif what == "sums":
                        block_sums(it, a)

            pe.sem_inc(s_score, NS * HPG)
            pe.sem_inc(s_ctx, NS)
            pe.wait_ge(s_const, 5)
            pe.wait_ge(s_one, 3)
            for u in range(NU):
                unit(0, u)
            rows(0)
            with pe.Fori(0, ITERS - 1) as it:
                walk(it, True)
            walk(ITERS - 1, False)

        @block.scalar
        def _(act):
            def exp(it, s, h):
                qb, kt = STEPS[s]
                q0 = max(0, kt * P - qb * BLK)
                act.wait_ge(s_score, (it + 1) * NS * HPG + (s * HPG + h + 1))
                if h == 0:
                    act.wait_ge(s_ctx, it * NS + (NS + s + 1 - RING))
                    if s >= RING:
                        qb0, kt0 = STEPS[s - RING]
                        if kt0 in ADDED[qb0]:
                            act.wait_ge(s_add, it * NADD + adds_before(qb0, kt0))
                act.activation(probs[s % RING][:, h, q0:BLK], ps_s[:, (s * HPG + h) % ST_BANKS, q0:BLK], ACT.Exp).then_inc(s_exp, 1)

            def take(it, qb):
                if ADDS[qb]:
                    act.wait_ge(s_sum, it * (QB - 1) + (2 + qb))
                else:
                    act.wait_ge(s_ctx, it * NS + (NS + ENDS[qb]))
                act.wait_ge(s_norm, it * QB + (qb + 1))
                act.activation(raw[qb % 2][:, :], ps_c[:, 0, :], ACT.Copy).then_inc(s_take, 1)
                act.activation(sums[qb % 2][:, :], ps_d[:, 0, :], ACT.Copy).then_inc(s_take, 1)

            def store(it, b, g, qb):
                act.wait_ge(s_hi, it * QB + (qb + 1))
                act.dma_start(d["ctx"][b, g, 0, :, bass.ts(qb, BLK)], out_hi[qb % 2][:, :].bitcast(F32)).then_inc(s_st[qb % 2], 16)
                act.wait_ge(s_lo, it * QB + (qb + 1))
                act.dma_start(d["ctx"][b, g, 1, :, bass.ts(qb, BLK)], out_lo[qb % 2][:, :].bitcast(F32)).then_inc(s_st[qb % 2], 16)

            def walk(it, b, g, maxima):
                for what, a, h in order(maxima):
                    if what == "scores":
                        exp(it, a, h)
                    elif what == "take":
                        take(it, a)
                    elif what == "store":
                        store(it, b, g, a)

            act.sem_inc(s_exp, ST_BANKS)
            act.sem_inc(s_take, 2)
            with act.Fori(0, ITERS - 1) as it:
                walk(it, it // GROUPS, it % GROUPS, True)
            walk(ITERS - 1, B - 1, GROUPS - 1, False)
            for r in range(2):
                act.wait_ge(s_st[r], 32 + 32 * ITERS * QB // 2)

        @block.vector
        def _(dve):
            def maximum(it, u):
                qt, h, c = UNITS[u]
                w, at = min(BLK, (qt + 1) * P - c * BLK), (qt // 4 * HPG + h) * 4 + qt % 4
                dve.wait_ge(s_unit, it * NU + (u + 1))
                dve.tensor_reduce(parts[:, at, c:c + 1], ps_m[:, u % M_BANKS, 0:w], AX.X, ALU.max).then_inc(s_taken, 1)

            def rows(it):
                dve.wait_ge(s_taken, it * UF + (M_BANKS + NU))
                dve.tensor_reduce(neg_max[:, 0:QB * HPG * 4], parts[:, :, :], AX.X, ALU.max, negate=True).then_inc(s_neg, 1)
                dve.wait_ge(s_rt, it + 1)
                for c in range(QB):
                    dve.wait_ge(s_row[c], it * 32 + 32)
                row = ps_m[0:QB * HPG * 4, 0, 0:P]
                dve.tensor_copy(rows_hi[:, :], row).then_inc(s_rhi, 1)
                dve.wait_ge(s_rhi, it + 1)
                dve.tensor_tensor(rows_lo[:, :], row, rows_hi[:, :], ALU.subtract).then_inc(s_rlo, 1)
                dve.wait_ge(s_rlo, it + 1)
                dve.sem_inc(s_taken, 1)

            def normalise(it, qb):
                n, r = it * QB + qb, qb % 2
                dve.wait_ge(s_take, it * 2 * QB + (2 + 2 * (qb + 1)))
                dve.reciprocal(inv[:, :], sums[r][:, :]).then_inc(s_inv, 1)
                dve.wait_ge(s_inv, n + 1)
                dve.tensor_tensor(out[:, :], raw[r][:, :], inv[:, :], ALU.mult).then_inc(s_norm, 1)
                dve.wait_ge(s_norm, n + 3)
                dve.wait_ge(s_st[r], it * 64 + 32 * (qb // 2 + 1))
                dve.tensor_copy(out_hi[r][:, :], out[:, :]).then_inc(s_hi, 1)
                dve.wait_ge(s_hi, n + 1)
                dve.tensor_tensor(out_lo[r][:, :], out[:, :], out_hi[r][:, :], ALU.subtract).then_inc(s_lo, 1)
                dve.wait_ge(s_lo, n + 1)

            def walk(it, maxima):
                for what, a, h in order(maxima):
                    if what == "maximum":
                        maximum(it + 1, a)
                    elif what == "rows":
                        rows(it + 1)
                    elif what == "normalise":
                        normalise(it, a)

            dve.sem_inc(s_taken, M_BANKS)
            dve.sem_inc(s_norm, 2)
            for sm in s_row + s_st:
                dve.sem_inc(sm, 32)
            dve.memset(parts[:, :, :], -3.0e38).then_inc(s_one, 1)
            dve.memset(neg_max[:, :], 0.0).then_inc(s_one, 1)
            dve.memset(k_e[QROWS:MROWS, :].bitcast(F32), 1.0).then_inc(s_one, 1)
            dve.wait_ge(s_one, 3)
            for u in range(NU):
                maximum(0, u)
            rows(0)
            with dve.Fori(0, ITERS - 1) as it:
                walk(it, True)
            walk(ITERS - 1, False)


def skewed(eng, parts, tiles, unroll=4):
    most = max(lag for lag, _ in parts)
    peeled = max(-(-most // unroll), 1)
    for k in range(peeled * unroll):
        for lag, part in parts:
            if k >= lag:
                part(k - lag, (k - lag) % unroll, (k - lag) // unroll)
    with eng.Fori(peeled, tiles // unroll) as i:
        for t in range(unroll):
            for lag, part in parts:
                part(i * unroll + (t - lag), (t - lag) % unroll, i + (t - lag) // unroll)
    for k in range(tiles, tiles + most):
        for lag, part in parts:
            if k - lag < tiles:
                part(k - lag, (k - lag) % unroll, (k - lag) // unroll)


R4 = 4
TT_ALL = TOK // P


def post(nc, sems, x, Wo, bo, gamma, beta, scale, d):
    with ExitStack() as ctx:
        al = Names(nc, ctx, sems)
        ring = lambda name, shape, dt=F32: [al.sbuf(f"p3_{name}{r}", shape, dt) for r in range(R4)]
        sem = lambda name: al.sem("p3_" + name)
        sem4 = lambda name: [al.sem(f"p3_{name}{r}") for r in range(R4)]
        ident = al.sbuf("p3_ident", [P, P])
        w_raw = al.sbuf("p3_w", [P, GROUPS, D])
        w_hi, w_lo = al.sbuf("p3_w_hi", [P, GROUPS, D], F32R), al.sbuf("p3_w_lo", [P, GROUPS, D], F32R)
        bo_r, gamma_r, beta_r = (al.sbuf(f"p3_{n}", [P, D]) for n in ("bo", "gamma", "beta"))
        scale_r = al.sbuf("p3_scale", [P, 1])
        c_hi, c_lo = ring("c_hi", [P, GROUPS, P], F32R), ring("c_lo", [P, GROUPS, P], F32R)
        x_in, x_b, y, x1 = ring("x", [P, D]), ring("xb", [P, D]), ring("y", [P, D]), ring("x1", [P, D])
        z, zg, xl, sq, xn = (ring(n, [P, D]) for n in ("z", "zg", "xl", "sq", "xn"))
        xt = ring("xt", [P, DC, P])
        n1, n2 = ring("n1", [P, 12]), ring("n2", [P, 12])
        l2 = ring("l2", [P, 5])
        ps_p, ps_t = al.psum("p3_ps_p", R4), al.psum("p3_ps_t", R4)

        s_id0, s_id, s_w, s_vec, s_whi, s_wlo = (sem(n) for n in ("id0", "id", "w", "vec", "w_hi", "w_lo"))
        s_c, s_x = sem4("c_in"), sem4("x_in")
        s_proj, s_xb, s_y, s_n1, s_d1, s_x1 = (sem(n) for n in ("proj", "xb", "y", "inv1", "dev1", "x1"))
        s_y2, s_n2, s_d2, s_z, s_g = (sem(n) for n in ("stats2", "inv2", "dev2", "z", "xl"))
        s_sq, s_nrm, s_inv, s_xn = (sem(n) for n in ("sumsq", "norm", "inv", "xn"))
        s_tr, s_xt = sem("transposed"), sem("xt")
        o_x1, o_xl, o_t = sem4("x1_out"), sem4("xl_out"), sem4("t_out")

        block = ctx.enter_context(nc.Block())
        x_d = x.rearrange("b n c -> (b n) c")

        @block.sync
        def _(sp):
            sp.dma_start(w_raw[:, :, :], Wo.rearrange("(g p) n -> p g n", p=P)).then_inc(s_w, 16)
            for dst, src in ((bo_r, bo), (gamma_r, gamma), (beta_r, beta), (scale_r, scale)):
                sp.dma_start(dst[:, :], src.partition_broadcast(P)).then_inc(s_vec, 16)

            def load(n, r, u):
                b, m = n // NT, n % NT
                sp.wait_ge(s_proj, n + 1)
                for half, dst in ((0, c_hi), (1, c_lo)):
                    sp.dma_start(dst[r][:, :, :].bitcast(F32), d["ctx"][b, :, half, :, bass.ds(m * P, P)]
                                 .rearrange("g p n -> p g n")).then_inc(s_c[r], 16)
                sp.wait_ge(s_xb, n + 1)
                sp.dma_start(x_in[r][:, :], x_d[bass.ds(n * P, P), :]).then_inc(s_x[r], 16)

            def store_x1(n, r, u):
                sp.wait_ge(s_x1, n + 1 + R4)
                sp.dma_start(d["x1"][bass.ds(n * P, P), :], x1[r][:, :]).then_inc(o_x1[r], 16)

            def store_xl(n, r, u):
                sp.wait_ge(s_g, n * 2 + (2 + 2 * R4))
                sp.dma_start(d["xl"][n, :, :], xl[r][:, :]).then_inc(o_xl[r], 16)

            def store_t(n, r, u):
                sp.wait_ge(s_xt, n + 1 + R4)
                sp.dma_start(d["xT"][n, :, :, :], xt[r][:, :, :]).then_inc(o_t[r], 16)

            skewed(sp, [(0, load), (2, store_x1), (5, store_xl), (9, store_t)], TT_ALL)
            for r in range(R4):
                sp.wait_ge(o_x1[r], 16 * (1 + TT_ALL // R4))
                sp.wait_ge(o_xl[r], 16 * (1 + TT_ALL // R4))
                sp.wait_ge(o_t[r], 16 * (1 + TT_ALL // R4))

        @block.gpsimd
        def _(pool):
            pool.memset(ident[:, :], 0.0).then_inc(s_id0, 1)
            pool.wait_ge(s_id0, 1)
            pool.affine_select(out=ident[:, :], in_=ident[:, :], compare_op=ALU.not_equal, fill=1.0,
                               base=0, pattern=[[-1, P]], channel_multiplier=1).then_inc(s_id, 1)
            pool.wait_ge(s_vec, 64)

            def add_bias(n, r, u):
                pool.wait_ge(s_x[r], u * 16 + 16)
                pool.wait_ge(s_y, n * 1 + 1)
                pool.tensor_tensor(x_b[r][:, :], x_in[r][:, :], bo_r[:, :], ALU.add).then_inc(s_xb, 1)

            def affine(n, r, u):
                pool.wait_ge(s_z, n + 1 + R4)
                pool.tensor_tensor(zg[r][:, :], z[r][:, :], gamma_r[:, :], ALU.mult).then_inc(s_g, 1)
                pool.wait_ge(s_g, n * 2 + (1 + 2 * R4))
                pool.wait_ge(s_xn, n + 1)
                pool.wait_ge(o_xl[r], u * 16 + 16)
                pool.tensor_tensor(xl[r][:, :], zg[r][:, :], beta_r[:, :], ALU.add).then_inc(s_g, 1)

            skewed(pool, [(0, add_bias), (4, affine)], TT_ALL)

        @block.tensor
        def _(pe):
            pe.sem_inc(s_proj, R4)
            pe.sem_inc(s_tr, R4)
            pe.wait_ge(s_wlo, 1)
            pe.wait_ge(s_id, 1)

            def project(n, r, u):
                pe.wait_ge(s_c[r], u * 32 + 32)
                pe.wait_ge(s_y, n + 1)
                for g in range(GROUPS):
                    mm = three_passes(pe, ps_p[:, r, :], c_hi[r][:, g, :], c_lo[r][:, g, :],
                                      w_hi[:, g, :], w_lo[:, g, :], g == 0, g == GROUPS - 1)
                mm.then_inc(s_proj, 1)

            def transpose(n, r, u):
                pe.wait_ge(s_xn, n + 1 + R4)
                pe.wait_ge(s_xt, n + 1)
                for c in range(DC):
                    mm = pe.transpose(ps_t[:, r, bass.ts(c, P)], xn[r][:, bass.ts(c, P)], ident[:, :])
                mm.then_inc(s_tr, 1)

            skewed(pe, [(0, project), (7, transpose)], TT_ALL)

        @block.scalar
        def _(act):
            for s in (s_x1, s_z, s_xn, s_xt):
                act.sem_inc(s, R4)

            def dev1(n, r, u):
                act.wait_ge(s_y, n + 1 + R4)
                act.wait_ge(s_n1, n * 2 + 2)
                act.activation(n1[r][:, 9:10], n1[r][:, 8:9], ACT.Sqrt).then_inc(s_d1, 1)

            def norm1(n, r, u):
                act.wait_ge(s_n1, n * 2 + (2 + 2 * R4))
                act.wait_ge(o_x1[r], u * 16 + 16)
                act.wait_ge(s_z, n + 1)
                act.activation(x1[r][:, :], y[r][:, :], ACT.Identity, scale=n1[r][:, 10:11], bias=n1[r][:, 11:12]).then_inc(s_x1, 1)

            def dev2(n, r, u):
                act.wait_ge(s_y2, n + 1)
                act.wait_ge(s_n2, n * 2 + 2)
                act.activation(n2[r][:, 9:10], n2[r][:, 8:9], ACT.Sqrt).then_inc(s_d2, 1)

            def norm2(n, r, u):
                act.wait_ge(s_n2, n * 2 + (2 + 2 * R4))
                act.wait_ge(s_g, n * 2 + 2)
                act.activation(z[r][:, :], x1[r][:, :], ACT.Identity, scale=n2[r][:, 10:11], bias=n2[r][:, 11:12]).then_inc(s_z, 1)

            def squares(n, r, u):
                act.wait_ge(s_g, n * 2 + (2 + 2 * R4))
                act.wait_ge(s_inv, n * 3 + 3)
                act.activation(sq[r][:, :], xl[r][:, :], ACT.Square, accum_out=l2[r][:, 0:1]).then_inc(s_sq, 1)
                act.wait_ge(s_sq, n + 1)
                act.activation(l2[r][:, 1:2], l2[r][:, 0:1], ACT.Sqrt).then_inc(s_nrm, 1)

            def unit_rows(n, r, u):
                act.wait_ge(s_inv, n * 3 + (3 + 3 * R4))
                act.wait_ge(s_tr, n + 1)
                act.activation(xn[r][:, :], xl[r][:, :], ACT.Copy, scale=l2[r][:, 4:5]).then_inc(s_xn, 1)

            def copy(n, r, u):
                act.wait_ge(s_tr, n + 1 + R4)
                act.wait_ge(o_t[r], u * 16 + 16)
                act.activation(xt[r][:, :, :], ps_t[:, r, :], ACT.Copy).then_inc(s_xt, 1)

            skewed(act, [(8, copy), (6, unit_rows), (5, squares), (3, norm2), (2, dev2), (1, norm1), (0, dev1)], TT_ALL)

        @block.vector
        def _(dve):
            dve.wait_ge(s_w, 16)
            dve.tensor_copy(w_hi[:, :, :], w_raw[:, :, :]).then_inc(s_whi, 1)
            dve.wait_ge(s_whi, 1)
            dve.tensor_tensor(w_lo[:, :, :], w_raw[:, :, :], w_hi[:, :, :], ALU.subtract).then_inc(s_wlo, 1)
            dve.wait_ge(s_vec, 64)
            dve.sem_inc(s_y, R4)
            dve.sem_inc(s_n1, 2 * R4)
            dve.sem_inc(s_n2, 2 * R4)
            dve.sem_inc(s_inv, 3 * R4)
            dve.sem_inc(s_xb, R4)
            dve.sem_inc(s_g, 2 * R4)
            for r in range(R4):
                dve.sem_inc(o_x1[r], 16)
                dve.sem_inc(o_xl[r], 16)
                dve.sem_inc(o_t[r], 16)
            steps = {k: al.sem(f"p3_dve_{k}") for k in ("a", "b", "c", "d")}

            def statistics(n, small, rows, s, out_sem):
                dve.bn_stats(small[:, 0:6], rows).then_inc(s, 1)
                dve.wait_ge(s, n * 3 + 1)
                dve.memset(small[:, 8:9], LN_EPS).then_inc(s, 1)
                dve.bn_aggr(small[:, 6:8], small[:, 0:6]).then_inc(s, 1)
                dve.wait_ge(s, n * 3 + 3)
                dve.tensor_tensor(small[:, 8:9], small[:, 7:8], small[:, 8:9], ALU.add).then_inc(out_sem, 1)

            def first(n, r, u):
                dve.wait_ge(s_proj, n + 1 + R4)
                dve.wait_ge(s_xb, n + 1 + R4)
                dve.wait_ge(s_x1, n + 1)
                dve.tensor_tensor(y[r][:, :], ps_p[:, r, :], x_b[r][:, :], ALU.add).then_inc(steps["a"], 1)
                dve.wait_ge(steps["a"], n + 1)
                statistics(n, n1[r], y[r][:, :], steps["b"], s_y)

            def inverse(n, small, s_dev, s_inv_):
                dve.wait_ge(s_dev, n + 1)
                dve.reciprocal(small[:, 10:11], small[:, 9:10]).then_inc(s_inv_, 1)
                dve.wait_ge(s_inv_, n * 2 + (1 + 2 * R4))
                dve.tensor_scalar(small[:, 11:12], small[:, 6:7], small[:, 10:11], -1.0, ALU.mult, ALU.mult).then_inc(s_inv_, 1)

            def inverse1(n, r, u):
                inverse(n, n1[r], s_d1, s_n1)

            def second(n, r, u):
                dve.wait_ge(s_x1, n + 1 + R4)
                statistics(n, n2[r], x1[r][:, :], steps["c"], s_y2)

            def inverse2(n, r, u):
                inverse(n, n2[r], s_d2, s_n2)

            def unit(n, r, u):
                dve.wait_ge(s_nrm, n + 1)
                dve.tensor_scalar_max(l2[r][:, 2:3], l2[r][:, 1:2], L2_EPS).then_inc(s_inv, 1)
                dve.wait_ge(s_inv, n * 3 + (1 + 3 * R4))
                dve.reciprocal(l2[r][:, 3:4], l2[r][:, 2:3]).then_inc(s_inv, 1)
                dve.wait_ge(s_inv, n * 3 + (2 + 3 * R4))
                dve.tensor_tensor(l2[r][:, 4:5], l2[r][:, 3:4], scale_r[:, :], ALU.mult).then_inc(s_inv, 1)

            skewed(dve, [(6, unit), (3, inverse2), (2, second), (1, inverse1), (0, first)], TT_ALL)


def slot_norms(nc, sems, mu, d):
    with ExitStack() as ctx:
        al = Names(nc, ctx, sems)
        sem = lambda name: al.sem("n_" + name)
        U = 4
        raw = [al.sbuf(f"n_mu{r}", [P, DC, S]) for r in range(U)]
        sq = [al.sbuf(f"n_sq{r}", [P, DC, S]) for r in range(U)]
        one = al.sbuf("n_one", [P, 1])
        norm, top, inv = (al.sbuf(f"n_{n}", [P, E]) for n in ("norm", "top", "inv"))
        ps = al.psum("n_ps", 1)
        s_in = [sem(f"in{r}") for r in range(U)]
        s_one, s_sq, s_sum, s_norm, s_top, s_inv, s_out = (sem(n) for n in ("one", "squared", "summed", "norm", "top", "inv", "out"))
        block = ctx.enter_context(nc.Block())
        mu_e = mu.rearrange("(c p) e s -> p e c s", p=P)

        @block.sync
        def _(sp):
            def load(e, r, u):
                sp.wait_ge(s_sq, e + 1)
                for c in range(DC):
                    sp.dma_start(raw[r][:, c, :], mu_e[:, bass.ds(e, 1), c, :].rearrange("p e s -> p (e s)")).then_inc(s_in[r], 16)

            skewed(sp, [(0, load)], E, U)
            sp.wait_ge(s_inv, 1)
            sp.dma_start(d["inv"], inv[:, :]).then_inc(s_out, 16)
            sp.wait_ge(s_out, 16)

        @block.tensor
        def _(pe):
            pe.sem_inc(s_sum, U)
            pe.wait_ge(s_one, 1)

            def total(e, r, u):
                pe.wait_ge(s_sq, e + 1 + U)
                for c in range(DC):
                    mm = pe.matmul(ps[:, 0, bass.ds(e, 1)], sq[r][:, c, :], one[:, :], start=c == 0, stop=c == DC - 1)
                mm.then_inc(s_sum, 1)

            skewed(pe, [(0, total)], E, U)

        @block.scalar
        def _(act):
            act.sem_inc(s_sq, U)

            def square(e, r, u):
                act.wait_ge(s_in[r], u * 16 * DC + 16 * DC)
                act.wait_ge(s_sum, e + 1)
                act.activation(sq[r][:, :, :], raw[r][:, :, :], ACT.Square).then_inc(s_sq, 1)

            skewed(act, [(0, square)], E, U)
            act.wait_ge(s_sum, E + U)
            act.activation(norm[:, :], ps[:, 0, 0:E], ACT.Sqrt).then_inc(s_norm, 1)

        @block.vector
        def _(dve):
            dve.memset(one[:, :], 1.0).then_inc(s_one, 1)
            dve.wait_ge(s_norm, 1)
            dve.tensor_scalar_max(top[:, :], norm[:, :], L2_EPS).then_inc(s_top, 1)
            dve.wait_ge(s_top, 1)
            dve.reciprocal(inv[:, :], top[:, :]).then_inc(s_inv, 1)


JG = 4
TG = NT // JG


def slots(nc, sems, mu, W1, b1_t, W2, b2, d):
    with ExitStack() as ctx:
        al = Names(nc, ctx, sems)
        sem = lambda name: al.sem("p4_" + name)
        pair = lambda name, shape: (al.sbuf(f"p4_{name}_lo", shape, F32R), al.sbuf(f"p4_{name}_hi", shape, F32R))
        xT_lo, xT_hi = pair("xT", [P, NT, DC, P])
        xl_lo, xl_hi = pair("xl", [P, NT, D])
        m_lo, m_hi = zip(*(pair(f"mu{r}", [P, DC, S]) for r in range(2)))
        w1_lo, w1_hi = pair("w1", [P, DC, H])
        w2_lo, w2_hi = pair("w2", [P, D])
        b1_c, inv_n = al.sbuf("p4_b1", [P, E]), al.sbuf("p4_inv_n", [P, E])
        m_raw, w1_raw, w2_raw = (al.sbuf(f"p4_{n}_raw", [P, D]) for n in ("mu", "w1", "w2"))
        own, own_b1 = [al.sbuf(f"p4_own{r}", [P, 1]) for r in range(2)], al.sbuf("p4_own_b1", [P, 1])
        b2_r = al.sbuf("p4_b2", [P, D])
        ident = al.sbuf("p4_ident", [P, P])
        logit = al.sbuf("p4_logit", [P, JG, BANK])
        ex = [al.sbuf(f"p4_ex{r}", [P, JG, BANK]) for r in range(2)]
        most = al.sbuf("p4_most", [P, JG, BANK])
        col = [al.sbuf(f"p4_col{r}", [P, 12]) for r in range(2)]
        eT_hi = [al.sbuf(f"p4_eT_hi{r}", [P, TG, S], F32R) for r in range(2)]
        eT_lo = [al.sbuf(f"p4_eT_lo{r}", [P, TG, S], F32R) for r in range(2)]
        si = al.sbuf("p4_si", [P, D])
        siT_hi, siT_lo = al.sbuf("p4_siT_hi", [P, DC, S], F32R), al.sbuf("p4_siT_lo", [P, DC, S], F32R)
        h = al.sbuf("p4_h", [P, S])
        h_hi, h_lo = al.sbuf("p4_h_hi", [P, S], F32R), al.sbuf("p4_h_lo", [P, S], F32R)
        so = si
        so_hi, so_lo = al.sbuf("p4_so_hi", [P, D], F32R), al.sbuf("p4_so_lo", [P, D], F32R)
        m_col, m_row = al.sbuf("p4_m_col", [P, P]), al.sbuf("p4_m_row", [NT, P])
        ps_l, ps_t, ps_s, ps_e = al.psum("p4_ps_l", JG), al.psum("p4_ps_t", 2), al.psum("p4_ps_s", 1), al.psum("p4_ps_e", 1)

        s_xT, s_xl = [sem(f"xT{j}") for j in range(JG)], [sem(f"xl{j}") for j in range(JG)]
        s_xThi, s_xTlo, s_xlhi, s_xllo = sem("xT_hi"), sem("xT_lo"), sem("xl_hi"), sem("xl_lo")
        s_mu, s_w, s_b2, s_vec = sem("mu"), sem("weights"), sem("b2"), sem("vectors")
        s_muhi, s_mulo, s_whi, s_wlo = sem("mu_hi"), sem("mu_lo"), sem("w_hi"), sem("w_lo")
        s_id0, s_id, s_reset, s_own = sem("id0"), sem("id"), sem("reset"), sem("own")
        s_log, s_cp, s_most, s_ex, s_max, s_neg = (sem(n) for n in ("logits", "copied", "most", "exp", "max", "negated"))
        s_sum, s_rs, s_tr, s_ehi, s_elo, s_prod = (sem(n) for n in ("sum", "inverse", "transposed", "e_hi", "e_lo", "product"))
        s_si, s_sT, s_sThi, s_sTlo = sem("slot_in"), sem("slot_in_t"), sem("slot_in_hi"), sem("slot_in_lo")
        s_h, s_g, s_hhi, s_hlo, s_o = sem("hidden"), sem("gelu"), sem("h_hi"), sem("h_lo"), sem("slot_out")
        s_add, s_ohi, s_olo = sem("biased"), sem("o_hi"), sem("o_lo")
        s_mt, s_mc, s_mr, s_mrow = sem("most_t"), sem("m_col"), sem("m_row_t"), sem("m_row")
        o_l, o_so, o_m = sem("logits_stored"), sem("slot_out_stored"), sem("maxima_stored")
        block = ctx.enter_context(nc.Block())
        U = 2
        mu_e = mu.rearrange("(c p) e s -> p e c s", p=P)
        w1_e = W1.rearrange("e (c p) h -> p e c h", p=P)
        group = lambda j: slice(j * TG, (j + 1) * TG)

        @block.sync
        def _(sp):
            sp.dma_start(b1_c[:, :], b1_t).then_inc(s_vec, 16)
            sp.dma_start(inv_n[:, :], d["inv"]).then_inc(s_vec, 16)

            with sp.Fori(0, B) as b:
                def load_mu(n, r, u):
                    g = b * E + n
                    sp.wait_ge(s_mulo, g + 1)
                    for c in range(DC):
                        sp.dma_start(m_raw[:, bass.ts(c, S)], mu_e[:, bass.ds(n, 1), c, :]
                                     .rearrange("p e s -> p (e s)")).then_inc(s_mu, 16)

                def store_logits(n, r, u):
                    g = b * E + n
                    sp.wait_ge(s_cp, g * JG + 2 * JG)
                    sp.dma_start(d["logit"][g], logit[:, :, :]).then_inc(o_l, 16)

                def load_weights(n, r, u):
                    g = b * E + n
                    sp.wait_ge(s_wlo, g * 2 + 2)
                    for c in range(DC):
                        sp.dma_start(w1_raw[:, bass.ts(c, H)], w1_e[:, bass.ds(n, 1), c, :]
                                     .rearrange("p e h -> p (e h)")).then_inc(s_w, 16)
                    sp.dma_start(w2_raw[:, :], W2[n]).then_inc(s_w, 16)
                    sp.wait_ge(s_add, g + 1)
                    sp.dma_start(b2_r[:, :], b2[n].partition_broadcast(P)).then_inc(s_b2, 16)

                def store_out(n, r, u):
                    g = b * E + n
                    sp.wait_ge(s_ohi, g + 1)
                    sp.dma_start(d["so"][b, 0, :, n, :], so_hi[:, :].bitcast(F32)).then_inc(o_so, 16)
                    sp.wait_ge(s_olo, g + 2)
                    sp.dma_start(d["so"][b, 1, :, n, :], so_lo[:, :].bitcast(F32)).then_inc(o_so, 16)

                skewed(sp, [(0, load_mu), (1, store_logits), (2, load_weights), (3, store_out)], E, U)
                sp.wait_ge(s_mrow, b + 1)
                sp.dma_start(d["top"][b], m_row[:, :]).then_inc(o_m, 16)
            sp.wait_ge(o_l, 16 + 16 * B * E)
            sp.wait_ge(o_so, 32 + 32 * B * E)
            sp.wait_ge(o_m, 16 + 16 * B)

        @block.gpsimd
        def _(pool):
            pool.memset(ident[:, :], 0.0).then_inc(s_id0, 1)
            pool.wait_ge(s_id0, 1)
            pool.affine_select(out=ident[:, :], in_=ident[:, :], compare_op=ALU.not_equal, fill=1.0,
                               base=0, pattern=[[-1, P]], channel_multiplier=1).then_inc(s_id, 1)
            for b in range(B):
                pool.wait_ge(s_mt, b * JG + JG)
                pool.memset(most[:, :, :], -3.0e38).then_inc(s_reset, 1)
                pool.wait_ge(s_tr, b * E * JG + 2 * JG)
                for j in range(JG):
                    if j >= 2:
                        pool.wait_ge(s_xTlo, b * JG + j - 1)
                    pool.dma_start(ex[j % 2][:, :, :], d["xT"][bass.ds(b * NT + j * TG, TG)]
                                   .rearrange("t p c n -> p t (c n)")).then_inc(s_xT[j], 16)
                for j in range(JG):
                    pool.wait_ge(s_xTlo, b * JG + JG)
                    if j > 0:
                        pool.wait_ge(s_xllo, b * JG + j)
                    pool.dma_start(ex[1][:, :, :], d["xl"][bass.ds(b * NT + j * TG, TG)]
                                   .rearrange("t p n -> p t n")).then_inc(s_xl[j], 16)

        @block.tensor
        def _(pe):
            pe.sem_inc(s_log, 2 * JG)
            pe.sem_inc(s_tr, 2 * JG)
            pe.sem_inc(s_prod, 2)
            pe.sem_inc(s_mt, JG)
            for s in (s_sT, s_h, s_o):
                pe.sem_inc(s, 1)
            pe.wait_ge(s_id, 1)
            with pe.Fori(0, B) as b:
                def logits(j):
                    def part(n, r, u):
                        g = b * E + n
                        if j == 0:
                            pe.wait_ge(s_mulo, g + 2)
                        if isinstance(n, int) and n == 0:
                            pe.wait_ge(s_xTlo, b * JG + (j + 1))
                        pe.wait_ge(s_cp, g * JG + (j + 1))
                        for c in range(DC):
                            mm = three_passes(pe, ps_l[:, j, :], m_hi[r][:, c, :], m_lo[r][:, c, :],
                                              xT_hi[:, group(j), c, :], xT_lo[:, group(j), c, :], c == 0, c == DC - 1)
                        mm.then_inc(s_log, 1)
                    return part

                def transpose(j):
                    def part(n, r, u):
                        g = b * E + n
                        pe.wait_ge(s_ex, g * JG + (j + 1 + JG))
                        pe.wait_ge(s_elo, g * JG + (j + 1))
                        for t in range(TG):
                            mm = pe.transpose(ps_t[:, j % 2, bass.ts(t, P)], ex[r][:, j, bass.ts(t, P)], ident[:, :])
                        mm.then_inc(s_tr, 1)
                    return part

                def product(j):
                    def part(n, r, u):
                        g = b * E + n
                        if isinstance(n, int) and n == 0:
                            pe.wait_ge(s_xllo, b * JG + (j + 1))
                        if j == 0:
                            pe.wait_ge(s_si, g + 1)
                        pe.wait_ge(s_elo, g * JG + (j + 1 + 2))
                        for t in range(TG):
                            mm = three_passes(pe, ps_s[:, 0, :], eT_hi[j % 2][:, t, :], eT_lo[j % 2][:, t, :],
                                              xl_hi[:, j * TG + t, :], xl_lo[:, j * TG + t, :],
                                              j == 0 and t == 0, j == JG - 1 and t == TG - 1)
                        mm.then_inc(s_prod, 1)
                    return part

                def slot_in_t(n, r, u):
                    g = b * E + n
                    pe.wait_ge(s_si, g + 2)
                    pe.wait_ge(s_add, g + 1)
                    for c in range(DC):
                        mm = pe.transpose(ps_e[:, 0, bass.ts(c, P)], si[:, bass.ts(c, P)], ident[:, :])
                    mm.then_inc(s_sT, 1)

                def hidden(n, r, u):
                    g = b * E + n
                    pe.wait_ge(s_wlo, g * 2 + 3)
                    pe.wait_ge(s_sTlo, g + 1)
                    for c in range(DC):
                        mm = three_passes(pe, ps_e[:, 0, 0:S], w1_hi[:, c, :], w1_lo[:, c, :],
                                          siT_hi[:, c, :], siT_lo[:, c, :], c == 0, c == DC - 1)
                    mm.then_inc(s_h, 1)

                def slot_out(n, r, u):
                    g = b * E + n
                    pe.wait_ge(s_wlo, g * 2 + 4)
                    pe.wait_ge(s_hlo, g + 2)
                    three_passes(pe, ps_e[:, 0, :], h_hi[:, :], h_lo[:, :], w2_hi[:, :], w2_lo[:, :], True, True).then_inc(s_o, 1)

                skewed(pe, [(1, logits(0)), (3, slot_in_t), (1, logits(1)), (1, logits(2)), (3, hidden), (1, logits(3)),
                            (2, transpose(0)), (2, transpose(1)), (3, slot_out), (2, product(0)), (2, transpose(2)),
                            (2, product(1)), (2, transpose(3)), (2, product(2)), (2, product(3))], E, U)
                for j in range(JG):
                    pe.wait_ge(s_most, b * E * JG + (E * JG + j + 1))
                    pe.wait_ge(s_cp, b * E * JG + (E * JG + j + 1))
                    for t in range(TG):
                        mm = pe.transpose(ps_l[:, j, bass.ts(t, P)], most[:, j, bass.ts(t, P)], ident[:, :])
                    mm.then_inc(s_mt, 1)
                pe.wait_ge(s_mc, b * JG + (JG + 1))
                pe.wait_ge(s_add, b * E + E + 1)
                pe.transpose(ps_e[:, 0, 0:P], m_col[:, :], ident[:, :]).then_inc(s_mr, 1)

        @block.scalar
        def _(act):
            act.sem_inc(s_cp, JG)
            act.sem_inc(s_ex, JG)
            act.sem_inc(s_si, 1)
            with act.Fori(0, B) as b:
                for j in range(JG):
                    act.wait_ge(s_xT[j], b * 16 + 16)
                    act.wait_ge(s_log, b * E * JG + 2 * JG)
                    act.activation(xT_hi[:, group(j), :, :], ex[j % 2][:, :, :].rearrange("p t (c n) -> p t c n", c=DC), ACT.Copy).then_inc(s_xThi, 1)

                def vectors_hi(n, r, u):
                    g = b * E + n
                    act.wait_ge(s_mu, g * 16 * DC + 16 * DC)
                    act.wait_ge(s_log, g * JG + JG)
                    act.activation(m_hi[r][:, :, :], m_raw[:, :], ACT.Copy).then_inc(s_muhi, 1)

                def rows_hi(n, r, u):
                    if isinstance(n, int) and n == 0:
                        for j in range(JG):
                            act.wait_ge(s_xl[j], b * 16 + 16)
                            act.wait_ge(s_prod, b * E * JG + 2)
                            act.activation(xl_hi[:, group(j), :], ex[1][:, :, :], ACT.Copy).then_inc(s_xlhi, 1)

                def copy(j):
                    def part(n, r, u):
                        g = b * E + n
                        act.wait_ge(s_log, g * JG + (j + 1 + 2 * JG))
                        act.wait_ge(s_most, g * JG + (j + 1))
                        act.wait_ge(s_ex, g * JG + (j + 1))
                        act.wait_ge(o_l, g * 16 + 16)
                        act.activation(logit[:, j, :], ps_l[:, j, :], ACT.Copy, scale=own[r][:, 0:1]).then_inc(s_cp, 1)
                    return part

                def exp(j):
                    def part(n, r, u):
                        g = b * E + n
                        act.wait_ge(s_neg, g + 1)
                        act.wait_ge(s_tr, g * JG + (j + 1))
                        if isinstance(n, int) and n == 1:
                            act.wait_ge(s_xllo, b * JG + JG)
                        act.activation(ex[r][:, j, :], logit[:, j, :], ACT.Exp, bias=col[r][:, 5:6],
                                       accum_out=col[r][:, 6 + j:7 + j]).then_inc(s_ex, 1)
                    return part

                def split_hi(j):
                    def part(n, r, u):
                        g = b * E + n
                        act.wait_ge(s_tr, g * JG + (j + 1 + 2 * JG))
                        act.wait_ge(s_prod, g * JG + (j + 1))
                        act.activation(eT_hi[j % 2][:, :, :], ps_t[:, j % 2, :], ACT.Copy).then_inc(s_ehi, 1)
                    return part

                def slot_in(n, r, u):
                    g = b * E + n
                    act.wait_ge(s_prod, g * JG + (JG + 2))
                    act.wait_ge(s_rs, g + 1)
                    act.wait_ge(s_sT, g + 1)
                    act.wait_ge(s_olo, g + 1)
                    act.activation(si[:, :], ps_s[:, 0, :], ACT.Copy, scale=col[r][:, 11:12]).then_inc(s_si, 1)

                def slot_in_hi(n, r, u):
                    g = b * E + n
                    act.wait_ge(s_sT, g + 2)
                    act.wait_ge(s_h, g + 1)
                    act.activation(siT_hi[:, :, :], ps_e[:, 0, :], ACT.Copy).then_inc(s_sThi, 1)

                def gelu(n, r, u):
                    g = b * E + n
                    act.wait_ge(s_h, g + 2)
                    act.wait_ge(s_hlo, g + 1)
                    act.activation(h[:, :], ps_e[:, 0, 0:S], ACT.Gelu, bias=own_b1[:, :]).then_inc(s_g, 1)
                    act.wait_ge(s_g, g + 2)
                    act.wait_ge(s_o, g + 1)
                    act.activation(h_hi[:, :], h[:, :], ACT.Copy).then_inc(s_hhi, 1)

                def out_hi(n, r, u):
                    g = b * E + n
                    act.wait_ge(s_add, g + 2)
                    act.wait_ge(o_so, g * 32 + 32)
                    act.activation(so_hi[:, :], so[:, :], ACT.Copy).then_inc(s_ohi, 1)

                def weights_hi(n, r, u):
                    g = b * E + n
                    act.wait_ge(s_w, g * (16 * (DC + 1)) + 16 * (DC + 1))
                    act.wait_ge(s_h, g + 1)
                    act.activation(w1_hi[:, :, :], w1_raw[:, :], ACT.Copy).then_inc(s_whi, 1)
                    act.wait_ge(s_o, g + 1)
                    act.activation(w2_hi[:, :], w2_raw[:, :], ACT.Copy).then_inc(s_whi, 1)

                skewed(act, [(3, slot_in), (1, copy(0)), (3, slot_in_hi), (1, copy(1)), (1, copy(2)), (3, gelu), (1, copy(3)),
                             (2, split_hi(0)), (2, split_hi(1)), (1, exp(0)), (1, exp(1)), (2, split_hi(2)),
                             (1, exp(2)), (1, exp(3)), (3, out_hi), (2, split_hi(3)), (1, rows_hi), (0, vectors_hi), (2, weights_hi)], E, U)
                act.wait_ge(s_mr, b + 1)
                act.wait_ge(o_m, b * 16 + 16)
                act.activation(m_row[:, :], ps_e[0:NT, 0, 0:P], ACT.Copy).then_inc(s_mrow, 1)

        @block.vector
        def _(dve):
            dve.sem_inc(s_most, JG)
            for s in (s_elo, s_wlo):
                dve.sem_inc(s, 2)
            for s in (s_mulo, s_olo):
                dve.sem_inc(s, 1)
            dve.sem_inc(s_hlo, 1)
            dve.sem_inc(s_g, 1)
            dve.sem_inc(s_add, 1)
            dve.wait_ge(s_vec, 32)
            dve.sem_inc(o_l, 16)
            dve.sem_inc(o_so, 32)
            dve.sem_inc(o_m, 16)
            dve.memset(m_col[:, :], 0.0).then_inc(s_mc, 1)
            with dve.Fori(0, B) as b:
                for j in range(JG):
                    dve.wait_ge(s_xThi, b * JG + (j + 1))
                    dve.tensor_tensor(xT_lo[:, group(j), :, :], ex[j % 2][:, :, :].rearrange("p t (c n) -> p t c n", c=DC),
                                      xT_hi[:, group(j), :, :], ALU.subtract).then_inc(s_xTlo, 1)

                def vectors_lo(n, r, u):
                    g = b * E + n
                    dve.wait_ge(s_muhi, g + 1)
                    dve.tensor_scalar(own[r][:, :], inv_n[:, bass.ds(n, 1)], 1.0, None, ALU.mult).then_inc(s_own, 1)
                    dve.tensor_tensor(m_lo[r][:, :, :], m_raw[:, :].rearrange("p (c s) -> p c s", c=DC), m_hi[r][:, :, :], ALU.subtract).then_inc(s_mulo, 1)

                def rows_lo(n, r, u):
                    if isinstance(n, int) and n == 0:
                        for j in range(JG):
                            dve.wait_ge(s_xlhi, b * JG + (j + 1))
                            dve.tensor_tensor(xl_lo[:, group(j), :], ex[1][:, :, :],
                                              xl_hi[:, group(j), :], ALU.subtract).then_inc(s_xllo, 1)

                def maximum(j):
                    def part(n, r, u):
                        g = b * E + n
                        dve.wait_ge(s_cp, g * JG + (j + 1 + JG))
                        dve.tensor_reduce(col[r][:, j:j + 1], logit[:, j, :], AX.X, ALU.max).then_inc(s_max, 1)
                        if j == JG - 1:
                            dve.wait_ge(s_max, g * (JG + 1) + JG)
                            dve.tensor_reduce(col[r][:, 4:5], col[r][:, 0:JG], AX.X, ALU.max).then_inc(s_max, 1)
                            dve.wait_ge(s_max, g * (JG + 1) + JG + 1)
                            dve.tensor_scalar(col[r][:, 5:6], col[r][:, 4:5], -1.0, None, ALU.mult).then_inc(s_neg, 1)
                    return part

                def largest(j):
                    def part(n, r, u):
                        g = b * E + n
                        if isinstance(n, int) and n == 0 and j == 0:
                            dve.wait_ge(s_reset, b + 1)
                        dve.wait_ge(s_most, g * JG + (j + 1))
                        dve.tensor_tensor(most[:, j, :], most[:, j, :], logit[:, j, :], ALU.max).then_inc(s_most, 1)
                    return part

                def total(n, r, u):
                    g = b * E + n
                    dve.wait_ge(s_ex, g * JG + 2 * JG)
                    dve.tensor_reduce(col[r][:, 10:11], col[r][:, 6:10], AX.X, ALU.add).then_inc(s_sum, 1)
                    dve.wait_ge(s_sum, g + 1)
                    dve.reciprocal(col[r][:, 11:12], col[r][:, 10:11]).then_inc(s_rs, 1)

                def split_lo(j):
                    def part(n, r, u):
                        g = b * E + n
                        dve.wait_ge(s_ehi, g * JG + (j + 1))
                        dve.tensor_tensor(eT_lo[j % 2][:, :, :], ps_t[:, j % 2, :].rearrange("p (t s) -> p t s", t=TG),
                                          eT_hi[j % 2][:, :, :], ALU.subtract).then_inc(s_elo, 1)
                    return part

                def slot_in_lo(n, r, u):
                    g = b * E + n
                    dve.wait_ge(s_sThi, g + 1)
                    dve.tensor_tensor(siT_lo[:, :, :], ps_e[:, 0, :].rearrange("p (c s) -> p c s", c=DC),
                                      siT_hi[:, :, :], ALU.subtract).then_inc(s_sTlo, 1)

                def hidden_lo(n, r, u):
                    g = b * E + n
                    dve.wait_ge(s_hhi, g + 1)
                    dve.tensor_tensor(h_lo[:, :], h[:, :], h_hi[:, :], ALU.subtract).then_inc(s_hlo, 1)

                def bias(n, r, u):
                    g = b * E + n
                    dve.wait_ge(s_b2, g * 16 + 16)
                    dve.wait_ge(s_o, g + 2)
                    dve.tensor_tensor(so[:, :], ps_e[:, 0, :], b2_r[:, :], ALU.add).then_inc(s_add, 1)

                def out_lo(n, r, u):
                    g = b * E + n
                    dve.wait_ge(s_ohi, g + 1)
                    dve.tensor_tensor(so_lo[:, :], so[:, :], so_hi[:, :], ALU.subtract).then_inc(s_olo, 1)

                def weights_lo(n, r, u):
                    g = b * E + n
                    dve.wait_ge(s_whi, g * 2 + 2)
                    dve.wait_ge(s_g, g + 1)
                    dve.tensor_scalar(own_b1[:, :], b1_c[:, bass.ds(n, 1)], 1.0, None, ALU.mult).then_inc(s_own, 1)
                    dve.tensor_tensor(w1_lo[:, :, :], w1_raw[:, :].rearrange("p (c h) -> p c h", c=DC), w1_hi[:, :, :], ALU.subtract).then_inc(s_wlo, 1)
                    dve.tensor_tensor(w2_lo[:, :], w2_raw[:, :], w2_hi[:, :], ALU.subtract).then_inc(s_wlo, 1)

                skewed(dve, [(3, slot_in_lo), (1, maximum(0)), (1, largest(0)), (1, maximum(1)), (1, largest(1)), (1, maximum(2)),
                             (3, hidden_lo), (1, maximum(3)), (2, split_lo(0)), (2, split_lo(1)), (3, bias),
                             (1, largest(2)), (2, split_lo(2)), (1, largest(3)), (1, total),
                             (3, out_lo), (2, split_lo(3)), (1, rows_lo), (0, vectors_lo), (2, weights_lo)], E, U)
                for j in range(JG):
                    dve.wait_ge(s_mt, b * JG + (j + 1 + JG))
                    dve.wait_ge(s_mr, b)
                    dve.tensor_reduce(m_col[:, group(j)], ps_l[:, j, :].rearrange("p (t s) -> p t s", t=TG), AX.X, ALU.max).then_inc(s_mc, 1)


def combine(nc, sems, out, d):
    with ExitStack() as ctx:
        al = Names(nc, ctx, sems)
        sem = lambda name: al.sem("p6_" + name)
        U = 4
        ring = lambda name, shape, dt=F32: [al.sbuf(f"p6_{name}{r}", shape, dt) for r in range(U)]
        so = al.sbuf("p6_so", [P, B, 2, E, D], F32R)
        top = al.sbuf("p6_top", [P, B, N])
        one, zero = al.sbuf("p6_one", [P, 1]), al.sbuf("p6_zero", [P, BANK])
        lg = ring("lg", [P, BANK])
        c_hi, c_lo = ring("c_hi", [P, BANK], F32R), ring("c_lo", [P, BANK], F32R)
        acc = al.sbuf("p6_acc", [P, BANK])
        x1, y, res = (al.sbuf(f"p6_{n}", [P, TG, D]) for n in ("x1", "y", "res"))
        inv = al.sbuf("p6_inv", [P, TG])
        n3 = ring("n3", [P, 12])
        ps_o, ps_s = al.psum("p6_ps_o", TG), al.psum("p6_ps_s", 1)
        s_so, s_vec = [sem(f"so{k}") for k in range(4)], sem("vectors")
        s_lg, s_x1 = [sem(f"lg{r}") for r in range(U)], sem("x1")
        s_one, s_sub, s_ex, s_hi, s_lo, s_acc = (sem(n) for n in ("one", "shifted", "exp", "c_hi", "c_lo", "acc"))
        s_out, s_tot, s_inv0, s_y = sem("out"), sem("totals"), sem("inverse"), sem("y")
        s_bn, s_eps, s_dev, s_inv, s_res = (sem(n) for n in ("bn", "eps", "dev", "inv"  , "res"))
        o_r = sem("stored")
        block = ctx.enter_context(nc.Block())
        STEPS = B * JG * E
        out_d = out.rearrange("b n c -> (b n) c")
        last = lambda part: lambda n, m, G: part(G) if m == E - 1 else None

        def load_slots(eng, b):
            for k in range(4):
                for half in range(2):
                    eng.dma_start(so[:, b, half, bass.ts(k, E // 4), :].bitcast(F32), d["so"][b, half, :, bass.ts(k, E // 4), :]).then_inc(s_so[k], 16)

        @block.sync
        def _(sp):
            def next_slots(n, m, G):
                if isinstance(n, int) and n == 0:
                    sp.wait_ge(s_out, U + E - 3)
                    load_slots(sp, 1)

            def load(n, m, G):
                r = m % U
                sp.wait_ge(s_lo, n + 1)
                sp.wait_ge(s_acc, n + 1)
                sp.dma_start(lg[r][:, :], d["logit"][G // JG * E + m, :, bass.ds(G % JG * BLK, BLK)]).then_inc(s_lg[r], 16)

            def load_x1(n, m, G):
                if m == 0:
                    sp.wait_ge(s_y, G * TG + TG)
                    sp.dma_start(x1[:, :, :], d["x1"][bass.ds(G * BLK, BLK), :].rearrange("(t p) c -> p t c", p=P)).then_inc(s_x1, 16)

            def store(G):
                sp.wait_ge(s_res, G * TG + 2 * TG)
                sp.dma_start(out_d[bass.ds(G * BLK, BLK), :].rearrange("(t p) c -> p t c", p=P), res[:, :, :]).then_inc(o_r, 16)

            for b in range(B):
                sp.dma_start(top[:, b, :], d["top"][b].rearrange("t p -> (t p)").partition_broadcast(P)).then_inc(s_vec, 16)
            skewed(sp, [(0, load), (4, load_x1), (10, last(store)), (E - 1, next_slots)], STEPS, E)
            sp.wait_ge(o_r, 16 + 16 * STEPS // E)

        @block.gpsimd
        def _(pool):
            pool.sem_inc(s_acc, U)
            pool.wait_ge(s_one, 2)

            def accumulate(n, m, G):
                r = m % U
                pool.wait_ge(s_ex, n + 1)
                if m == 0:
                    pool.wait_ge(s_tot, G + 1)
                pool.wait_ge(s_acc, n + U)
                pool.tensor_tensor(acc[:, :], zero[:, :] if m == 0 else acc[:, :], lg[r][:, :], ALU.add).then_inc(s_acc, 1)

            skewed(pool, [(0, accumulate)], STEPS, E)

        @block.tensor
        def _(pe):
            pe.sem_inc(s_out, U)
            pe.sem_inc(s_tot, 1)

            def product(n, m, G):
                b, r = G // JG, m % U
                if m % 4 == 0:
                    pe.wait_ge(s_so[m // 4], b * 32 + 32)
                pe.wait_ge(s_lo, n + 1 + U)
                for t in range(TG):
                    if m == 0:
                        pe.wait_ge(s_y, G * TG + (t + 1))
                    rhs = [so[:, bass.ds(b, 1), half, m, :].rearrange("p b n -> p (b n)") for half in range(2)]
                    mm = three_passes(pe, ps_o[:, t, :], c_hi[r][:, bass.ts(t, P)], c_lo[r][:, bass.ts(t, P)], rhs[0], rhs[1],
                                      m == 0, m == E - 1)
                mm.then_inc(s_out, 1)

            def totals(G):
                pe.wait_ge(s_acc, G * E + (E + U))
                pe.wait_ge(s_inv0, G + 1)
                for t in range(TG):
                    mm = pe.matmul(ps_s[:, 0, t:t + 1], acc[:, bass.ts(t, P)], one[:, :], start=True, stop=True)
                mm.then_inc(s_tot, 1)

            pe.wait_ge(s_one, 1)
            skewed(pe, [(0, product), (0, last(totals))], STEPS, E)

        @block.scalar
        def _(act):
            act.sem_inc(s_res, TG)
            load_slots(act, 0)

            def exp(n, m, G):
                r = m % U
                act.wait_ge(s_sub, n + 1)
                act.activation(lg[r][:, :], lg[r][:, :], ACT.Exp).then_inc(s_ex, 1)
                act.wait_ge(s_ex, n + 1)
                act.wait_ge(s_out, n + 1)
                act.activation(c_hi[r][:, :], lg[r][:, :], ACT.Copy).then_inc(s_hi, 1)

            def deviation(t):
                def part(G):
                    act.wait_ge(s_eps, G * TG + (t + 1))
                    act.activation(n3[t][:, 9:10], n3[t][:, 8:9], ACT.Sqrt).then_inc(s_dev, 1)
                return last(part)

            def result(G):
                for t in range(TG):
                    act.wait_ge(s_inv, G * 2 * TG + 2 * (t + 1))
                    act.wait_ge(o_r, G * 16 + 16)
                    act.activation(res[:, t, :], y[:, t, :], ACT.Identity, scale=n3[t][:, 10:11], bias=n3[t][:, 11:12]).then_inc(s_res, 1)

            skewed(act, [(0, exp)] + [(6, deviation(t)) for t in range(TG)] + [(7, last(result))], STEPS, E)

        @block.vector
        def _(dve):
            dve.sem_inc(s_lo, U)
            dve.sem_inc(s_y, TG)
            dve.sem_inc(s_inv0, 1)
            dve.sem_inc(o_r, 16)
            dve.memset(one[:, :], 1.0).then_inc(s_one, 1)
            dve.memset(zero[:, :], 0.0).then_inc(s_one, 1)
            dve.wait_ge(s_vec, 16 * B)

            def shift(n, m, G):
                r = m % U
                dve.wait_ge(s_lg[r], G * (16 * E // U) + (m // U * 16 + 16))
                dve.tensor_tensor(lg[r][:, :], lg[r][:, :], top[:, bass.ds(G // JG, 1), bass.ds(G % JG * BLK, BLK)]
                                  .rearrange("p b n -> p (b n)"), ALU.subtract).then_inc(s_sub, 1)

            def split_lo(n, m, G):
                r = m % U
                dve.wait_ge(s_hi, n + 1)
                dve.tensor_tensor(c_lo[r][:, :], lg[r][:, :], c_hi[r][:, :], ALU.subtract).then_inc(s_lo, 1)

            def residual(G):
                dve.wait_ge(s_tot, G + 2)
                dve.reciprocal(inv[:, :], ps_s[:, 0, 0:TG]).then_inc(s_inv0, 1)
                dve.wait_ge(s_inv0, G + 2)
                dve.wait_ge(s_x1, G * 16 + 16)
                dve.wait_ge(s_res, G * TG + TG)
                for t in range(TG):
                    dve.scalar_tensor_tensor(y[:, t, :], ps_o[:, t, :], inv[:, t:t + 1], x1[:, t, :], ALU.mult, ALU.add).then_inc(s_y, 1)

            def statistics(t):
                def part(G):
                    small = n3[t]
                    dve.wait_ge(s_y, G * TG + (t + 1 + TG))
                    dve.bn_stats(small[:, 0:6], y[:, t, :]).then_inc(s_bn, 1)
                    dve.wait_ge(s_bn, G * 3 * TG + (3 * t + 1))
                    dve.memset(small[:, 8:9], LN_EPS).then_inc(s_bn, 1)
                    dve.bn_aggr(small[:, 6:8], small[:, 0:6]).then_inc(s_bn, 1)
                    dve.wait_ge(s_bn, G * 3 * TG + (3 * t + 3))
                    dve.tensor_tensor(small[:, 8:9], small[:, 7:8], small[:, 8:9], ALU.add).then_inc(s_eps, 1)
                return last(part)

            def inverse(G):
                for t in range(TG):
                    small = n3[t]
                    dve.wait_ge(s_dev, G * TG + (t + 1))
                    dve.reciprocal(small[:, 10:11], small[:, 9:10]).then_inc(s_inv, 1)
                    dve.wait_ge(s_inv, G * 2 * TG + (2 * t + 1))
                    dve.tensor_scalar(small[:, 11:12], small[:, 6:7], small[:, 10:11], -1.0, ALU.mult, ALU.mult).then_inc(s_inv, 1)

            skewed(dve, [(0, shift), (1, split_lo), (1, last(residual))]
                   + [(2 + t, statistics(t)) for t in range(TG)] + [(6, last(inverse))], STEPS, E)


def layer(nc, x, Wq, Wk, Wv, Wo, bo, gamma, beta, mu, scale, W1, b1_t, W2, b2, out):
    def scratch(name, shape):
        return nc.dram_tensor(name, shape, F32).ap()

    d = {
        "q": scratch("q_t", [B, GROUPS, 2, P, N]),
        "k": scratch("k_t", [B, 2, P, N]),
        "v": scratch("v", [TOK, P]),
        "ctx": scratch("ctx_t", [B, GROUPS, 2, P, N]),
        "x1": scratch("x1", [TOK, D]),
        "xl": scratch("x_ln", [TT_ALL, P, D]),
        "xT": scratch("x_unit_t", [TT_ALL, P, DC, P]),
        "inv": scratch("slot_norm", [P, E]),
        "logit": scratch("logits_t", [B * E, P, N]),
        "top": scratch("largest_logit", [B, NT, P]),
        "so": scratch("slot_out", [B, 2, P, E, D]),
    }
    stages = (
        lambda sems: projections(nc, sems, x, Wq, Wk, Wv, d),
        lambda sems: attention(nc, sems, d),
        lambda sems: post(nc, sems, x, Wo, bo, gamma, beta, scale, d),
        lambda sems: slot_norms(nc, sems, mu, d),
        lambda sems: slots(nc, sems, mu, W1, b1_t, W2, b2, d),
        lambda sems: combine(nc, sems, out, d),
    )
    for stage in stages:
        sems = []
        stage(sems)
        nc.clear_and_free_semaphores(sems)
        nc.all_engine_barrier()


_INS = ["L0_attn_x", "L0_attn_Wq", "L0_attn_Wk", "L0_attn_Wv", "L0_attn_Wo", "L0_attn_bo", "L0_ffn_gamma", "L0_ffn_beta",
        "L0_ffn_mu", "L0_ffn_scale", "L0_ffn_W1", "L0_ffn_b1", "L0_ffn_W2", "L0_ffn_b2"]


def kernel(**inputs):
    import concourse.bacc as bacc
    from concourse.bass_utils import run_bass_kernel_spmd

    nc = bacc.Bacc("TRN2", target_bir_lowering=False, num_devices=1)
    arrays, args = {}, []
    for name in _INS:
        a = np.ascontiguousarray(inputs[name].T if name == "L0_ffn_b1" else inputs[name])
        arrays[name + "_dram"] = a
        args.append(nc.dram_tensor(name + "_dram", a.shape, mybir.dt.from_np(a.dtype), kind="ExternalInput").ap())
    out = nc.dram_tensor("out_dram", [B, N, D], F32, kind="ExternalOutput").ap()
    layer(nc, *args, out)
    r = run_bass_kernel_spmd(nc, [arrays], core_ids=[0])
    return r.results[0]["out_dram"]
```

```python
import concourse.bass as bass
from concourse import mybir
from contextlib import ExitStack
import numpy as np

F32 = mybir.dt.float32
F32R = mybir.dt.float32r
BF16 = mybir.dt.bfloat16
ALU = mybir.AluOpType
ACT = mybir.ActivationFunctionType
AX = mybir.AxisListType

P = 128
BANK = 512
B, N, D = 2, 2048, 512
HEADS, GROUPS, HD = 16, 4, 32
HPG = HEADS // GROUPS
E, S, H = 16, 128, 128
DC = D // P
TOK = B * N
BLK = 512
NBLK = TOK // BLK
NT = N // P
QB = N // BLK
ITERS = B * GROUPS
SCALE = float(np.float32(1.0) / np.sqrt(np.float32(HD)))
MASKED = -1.0e38
LN_EPS = 1e-5
L2_EPS = 1e-12
QKV = HEADS * HD + 2 * GROUPS * HD
QROWS = 3 * HD
MROWS = QROWS + 2


class Names:

    def __init__(self, nc, ctx, sems):
        self.nc, self.ctx, self.sems = nc, ctx, sems

    def sbuf(self, name, shape, dt=F32):
        return self.ctx.enter_context(self.nc.sbuf_tensor(name, shape, dt))

    def psum(self, name, banks):
        return self.ctx.enter_context(self.nc.psum_tensor(name, [P, banks, BANK], F32))

    def sem(self, name):
        handle = self.nc.alloc_semaphore(name=name)
        self.sems.append(handle)
        return handle


def three_passes(pe, out, w_hi, w_lo, m_hi, m_lo, start, stop):
    pe.matmul(out, w_hi, m_hi, start=start, stop=False)
    pe.matmul(out, w_hi, m_lo, start=False, stop=False)
    return pe.matmul(out, w_lo, m_hi, start=False, stop=stop)


def projections(nc, sems, x, Wq, Wk, Wv, d):
    with ExitStack() as ctx:
        al = Names(nc, ctx, sems)
        ident = al.sbuf("p1_ident", [P, P])
        w_raw = al.sbuf("p1_w", [P, DC, QKV])
        w_hi = al.sbuf("p1_w_hi", [P, DC, QKV], F32R)
        w_lo = al.sbuf("p1_w_lo", [P, DC, QKV], F32R)
        x_in = [al.sbuf(f"p1_x{j}", [P, 4, D]) for j in range(2)]
        xT_hi = [al.sbuf(f"p1_xT_hi{j}", [P, DC, BLK], F32R) for j in range(2)]
        xT_lo = [al.sbuf(f"p1_xT_lo{j}", [P, DC, BLK], F32R) for j in range(2)]
        NF = GROUPS + 1
        f_hi = al.sbuf("p1_f_hi", [P, NF, BLK], F32R)
        f_lo = al.sbuf("p1_f_lo", [P, NF, BLK], F32R)
        FB, F0 = NF + 1, 4
        v_out = [al.sbuf(f"p1_v{j}", [P, 4, P]) for j in range(2)]
        ps_t = al.psum("p1_ps_t", DC)
        ps_f = al.psum("p1_ps_f", 4)

        s_ident0, s_ident = al.sem("p1_ident0"), al.sem("p1_ident")
        s_w, s_whi, s_wlo = al.sem("p1_w"), al.sem("p1_whi"), al.sem("p1_wlo")
        s_x = [al.sem(f"p1_x_loaded{j}") for j in range(2)]
        s_xt, s_xhi, s_xlo = al.sem("p1_transposed"), al.sem("p1_x_hi"), al.sem("p1_x_lo")
        s_f, s_fhi, s_flo = al.sem("p1_features"), al.sem("p1_f_hi"), al.sem("p1_f_lo_and_v")
        s_ohi = [al.sem(f"p1_stored_hi{m}") for m in range(NF)]
        s_olo = [al.sem(f"p1_stored_lo{m}") for m in range(NF)]
        s_ov = [al.sem(f"p1_stored_v{j}") for j in range(2)]

        block = ctx.enter_context(nc.Block())
        x_b = x.rearrange("b n c -> (b n) c")

        @block.sync
        def _(sp):
            for w, a, z in ((Wq, 0, D), (Wk, D, D + P), (Wv, D + P, QKV)):
                sp.dma_start(w_raw[:, :, a:z], w.rearrange("(c p) n -> p c n", p=P)).then_inc(s_w, 16)

            def load(blk, j):
                sp.dma_start(x_in[j][:, :, :], x_b[bass.ds(blk * BLK, BLK), :]
                             .rearrange("(t p) c -> p t c", p=P)).then_inc(s_x[j], 16)

            def store(blk, j):
                b, cols = blk // QB, bass.ds(blk % QB * BLK, BLK)
                for m in range(NF):
                    for half, src, done in ((0, f_hi, s_ohi), (1, f_lo, s_olo)):
                        if half == 0:
                            sp.wait_ge(s_fhi, blk * NF + (m + 1))
                        else:
                            sp.wait_ge(s_flo, blk * FB + (F0 + m + 1))
                        to = d["q"][b, m, half, :, cols] if m < GROUPS else d["k"][b, half, :, cols]
                        sp.dma_start(to, src[:, m, :].bitcast(F32)).then_inc(done[m], 16)
                sp.wait_ge(s_flo, blk * FB + (F0 + FB))
                sp.dma_start(d["v"][bass.ds(blk * BLK, BLK), :].rearrange("(t p) n -> p t n", p=P), v_out[j][:, :, :]).then_inc(s_ov[j], 16)

            for j in range(2):
                load(j, j)
            with sp.Fori(0, NBLK // 2 - 1) as i:
                at = i * 2
                for j in range(2):
                    store(at + j, j)
                    load(at + (j + 2), j)
            for j in range(2):
                store(NBLK - 2 + j, j)
            for m in range(NF):
                sp.wait_ge(s_ohi[m], 16 + 16 * NBLK)
                sp.wait_ge(s_olo[m], 16 + 16 * NBLK)
            for j in range(2):
                sp.wait_ge(s_ov[j], 16 + 16 * NBLK // 2)

        @block.gpsimd
        def _(pool):
            pool.memset(ident[:, :], 0.0).then_inc(s_ident0, 1)
            pool.wait_ge(s_ident0, 1)
            pool.affine_select(out=ident[:, :], in_=ident[:, :], compare_op=ALU.not_equal, fill=1.0,
                               base=0, pattern=[[-1, P]], channel_multiplier=1).then_inc(s_ident, 1)

        @block.tensor
        def _(pe):
            pe.wait_ge(s_ident, 1)
            pe.wait_ge(s_whi, 1)
            pe.wait_ge(s_wlo, 1)

            def transposes(blk, j, n):
                pe.wait_ge(s_x[j], n * 16 + 16)
                for c in range(DC):
                    pe.wait_ge(s_xlo, blk * DC + (c + 1))
                    for t in range(4):
                        last = pe.transpose(ps_t[:, c, t * P:(t + 1) * P], x_in[j][:, t, c * P:(c + 1) * P], ident[:, :])
                    last.then_inc(s_xt, 1)

            def features(blk, j, ms):
                for m in ms:
                    bank = (FB * j + m) % 4
                    if m == 0:
                        pe.wait_ge(s_xlo, blk * DC + 2 * DC)
                    pe.wait_ge(s_flo, blk * FB + (m + 1))
                    if m < NF:
                        for c in range(DC):
                            w = bass.ts(m, P)
                            last = three_passes(pe, ps_f[:, bank, :], w_hi[:, c, w], w_lo[:, c, w],
                                                xT_hi[j][:, c, :], xT_lo[j][:, c, :], c == 0, c == DC - 1)
                    else:
                        for t in range(4):
                            for c in range(DC):
                                w, n = bass.ts(m, P), bass.ts(t, P)
                                last = three_passes(pe, ps_f[:, bank, n], xT_hi[j][:, c, n], xT_lo[j][:, c, n],
                                                    w_hi[:, c, w], w_lo[:, c, w], c == 0, c == DC - 1)
                    last.then_inc(s_f, 1)

            def pair(at, half, ends):
                features(at, 0, range(0, 2))
                transposes(at + 1, 1, half)
                features(at, 0, range(2, FB))
                features(at + 1, 1, range(0, 2))
                if not ends:
                    transposes(at + 2, 0, half + 1)
                features(at + 1, 1, range(2, FB))

            transposes(0, 0, 0)
            with pe.Fori(0, NBLK // 2 - 1) as i:
                pair(i * 2, i, False)
            pair(NBLK - 2, NBLK // 2 - 1, True)

        @block.scalar
        def _(act):
            def split_hi(blk, j):
                act.wait_ge(s_f, blk * FB + FB)
                for c in range(DC):
                    act.wait_ge(s_xt, blk * DC + (c + 1))
                    act.activation(xT_hi[j][:, c, :], ps_t[:, c, :], ACT.Copy).then_inc(s_xhi, 1)

            def features_hi(blk, j, ms):
                for m in ms:
                    act.wait_ge(s_f, blk * FB + (2 * FB + m + 1))
                    act.wait_ge(s_ohi[m], blk * 16 + 16)
                    act.activation(f_hi[:, m, :], ps_f[:, (FB * j + m) % 4, :], ACT.Copy,
                                   scale=SCALE if m < GROUPS else 1.0).then_inc(s_fhi, 1)

            def pair(at, ends):
                features_hi(at, 0, range(0, 2))
                split_hi(at + 1, 1)
                features_hi(at, 0, range(2, NF))
                features_hi(at + 1, 1, range(0, 2))
                if not ends:
                    split_hi(at + 2, 0)
                features_hi(at + 1, 1, range(2, NF))

            split_hi(0, 0)
            with act.Fori(0, NBLK // 2 - 1) as i:
                pair(i * 2, False)
            pair(NBLK - 2, True)

        @block.vector
        def _(dve):
            dve.sem_inc(s_xlo, DC)
            dve.sem_inc(s_flo, F0)
            dve.sem_inc(s_f, 2 * FB)
            for done in s_ohi + s_olo + s_ov:
                dve.sem_inc(done, 16)
            dve.wait_ge(s_w, 48)
            dve.tensor_copy(w_hi[:, :, :], w_raw[:, :, :]).then_inc(s_whi, 1)
            dve.wait_ge(s_whi, 1)
            dve.tensor_tensor(w_lo[:, :, :], w_raw[:, :, :], w_hi[:, :, :], ALU.subtract).then_inc(s_wlo, 1)

            def split_lo(blk, j):
                for c in range(DC):
                    dve.wait_ge(s_xhi, blk * DC + (c + 1))
                    dve.tensor_tensor(xT_lo[j][:, c, :], ps_t[:, c, :], xT_hi[j][:, c, :], ALU.subtract).then_inc(s_xlo, 1)

            def features_lo(blk, j, ms):
                for m in ms:
                    dve.wait_ge(s_fhi, blk * NF + (m + 1))
                    dve.wait_ge(s_olo[m], blk * 16 + 16)
                    dve.scalar_tensor_tensor(out=f_lo[:, m, :], in0=ps_f[:, (FB * j + m) % 4, :],
                                             scalar=SCALE if m < GROUPS else 1.0, in1=f_hi[:, m, :],
                                             op0=ALU.mult, op1=ALU.subtract).then_inc(s_flo, 1)

            def values(blk, j, half):
                dve.wait_ge(s_f, blk * FB + 3 * FB)
                dve.wait_ge(s_ov[j], half * 16 + 16)
                dve.tensor_copy(v_out[j][:, :, :], ps_f[:, (FB * j + NF) % 4, :]).then_inc(s_flo, 1)

            def pair(at, half, ends):
                features_lo(at, 0, range(0, 2))
                split_lo(at + 1, 1)
                features_lo(at, 0, range(2, NF))
                values(at, 0, half)
                features_lo(at + 1, 1, range(0, 2))
                if not ends:
                    split_lo(at + 2, 0)
                features_lo(at + 1, 1, range(2, NF))
                values(at + 1, 1, half)

            split_lo(0, 0)
            with dve.Fori(0, NBLK // 2 - 1) as i:
                pair(i * 2, i, False)
            pair(NBLK - 2, NBLK // 2 - 1, True)


LAG = 2
RING = 4
M_BANKS, ST_BANKS = 3, 3
STEPS = [(qb, kt) for qb in range(QB) for kt in range(4 * (qb + 1))]
NS = len(STEPS)
ENDS = [4 * (qb + 1) * (qb + 2) // 2 for qb in range(QB)]
UNITS = [(qt, h, c) for qt in range(NT) for h in range(HPG) for c in range(qt // 4 + 1)]
NU = len(UNITS)
M_FROM, M_TO = 3, 35
ADDED = [[kt for kt in range(4 * qb) if kt % 4 != 0] for qb in range(QB)]
ADDS = [max(len(a) - 1, 0) for a in ADDED]
NADD = sum(ADDS)


def adds_before(qb, kt):
    return sum(ADDS[:qb]) + max(ADDED[qb].index(kt), 1)


def order(maxima):
    work, u = [], 0
    per = -(-NU // (M_TO - M_FROM))
    ends = {e - 1: qb for qb, e in enumerate(ENDS)}
    for s in range(NS + LAG + 5):
        for h in range(HPG):
            if s < NS:
                work.append(("scores", s, h))
            if h == 1 and LAG <= s < NS + LAG:
                work.append(("context", s - LAG, None))
                if s - LAG in ends:
                    work.append(("sums", ends[s - LAG], None))
            if maxima and M_FROM <= s < M_TO:
                for _ in range(per // HPG + (h < per % HPG)):
                    if u < NU:
                        work.append(("maximum", u, None))
                        u += 1
        if maxima and s == M_TO:
            work.append(("rows", None, None))
        if s - LAG in ends:
            work.append(("take", ends[s - LAG], None))
        for k in range(4):
            if s - LAG - k in ends:
                work.append(("inverse", ends[s - LAG - k], k))
        if s - LAG - 4 in ends:
            work.append(("normalise", ends[s - LAG - 4], None))
    return work


def attention(nc, sems, mu, d):
    with ExitStack() as ctx:
        al = Names(nc, ctx, sems)
        ident = al.sbuf("p2_ident", [P, P])
        ident_b = al.sbuf("p2_ident_b", [P, P], BF16)
        mask_kq = al.sbuf("p2_mask_kq", [P, P], BF16)
        mask_qk = al.sbuf("p2_mask_qk", [P, P], BF16)
        ones = al.sbuf("p2_ones", [P, HD])
        q_m = al.sbuf("p2_q_m", [QROWS, QB, HPG, BLK], F32R)
        k_m = al.sbuf("p2_k_m", [QROWS, N], F32R)
        q_e = al.sbuf("p2_q_e", [MROWS, QB, HPG, BLK], F32R)
        k_e = al.sbuf("p2_k_e", [MROWS, N], F32R)
        v_e = al.sbuf("p2_v", [P, NT, HD])
        parts = al.sbuf("p2_parts", [P, QB * HPG * 4, QB])
        neg_max = al.sbuf("p2_neg_max", [P, P])
        rows_hi = al.sbuf("p2_rows_hi", [QB * HPG * 4, P], F32R)
        rows_lo = al.sbuf("p2_rows_lo", [QB * HPG * 4, P], F32R)
        probs = [al.sbuf(f"p2_probs{r}", [P, HPG, BLK]) for r in range(RING)]
        added = [al.sbuf(f"p2_added{r}", [P, HPG, BLK]) for r in range(2)]
        raw = [al.sbuf(f"p2_raw{r}", [P, BLK]) for r in range(2)]
        sums = [al.sbuf(f"p2_sums{r}", [P, BLK]) for r in range(2)]
        inv = al.sbuf("p2_inv", [P, BLK])
        out = [al.sbuf(f"p2_out{r}", [P, BLK]) for r in range(2)]
        n_len, n_max, n_inv = (al.sbuf(f"p2_{n}", [P, E]) for n in ("slot_length", "slot_max", "slot_inv"))
        ps_s = al.psum("p2_ps_s", ST_BANKS)
        ps_m = al.psum("p2_ps_m", M_BANKS)
        ps_c = al.psum("p2_ps_c", 1)
        ps_d = al.psum("p2_ps_d", 1)

        sem = lambda name: al.sem("p2_" + name)
        s_const, s_const0, s_one = sem("const"), sem("const0"), sem("one")
        s_qm, s_km = [sem(f"q_m{c}") for c in range(QB)], [sem(f"k_m{c}") for c in range(QB)]
        s_qe, s_ke = [sem(f"q_e{c}") for c in range(QB)], [sem(f"k_e{c}") for c in range(QB)]
        s_ve, s_row = [sem(f"v{c}") for c in range(QB)], [sem(f"rows{c}") for c in range(QB)]
        s_unit = sem("unit_scored")
        s_taken = sem("unit_taken")
        s_neg, s_rt = sem("neg_max"), sem("rows_transposed")
        s_rhi, s_rlo = sem("rows_hi"), sem("rows_lo")
        s_score = sem("scored")
        s_exp = sem("exp")
        s_ctx = sem("context")
        s_add = sem("added")
        s_sum = sem("summed")
        s_take = sem("raw_taken")
        s_inv, s_norm = sem("inverse"), sem("normalised")
        s_st = [sem(f"ctx_stored{r}") for r in range(2)]

        s_nin, s_nsq, s_nadd, s_nsum, s_nlen, s_ninv, s_nout = (
            sem(n) for n in ("mu_in", "mu_squared", "mu_added", "mu_summed", "slot_length", "slot_inv", "slot_inv_stored"))
        EQ = E // RING

        block = ctx.enter_context(nc.Block())
        UF = NU + 1

        @block.sync
        def _(sp):
            def stacks(qs, ks, s_q, s_k, b, g, c, what):
                n = bass.ts(c, BLK)
                for r in range(3):
                    rows = slice(r * HD, (r + 1) * HD)
                    if "k" in what:
                        sp.dma_start(ks[rows, n].bitcast(F32), d["k"][b, int(r == 2), bass.ds(g * HD, HD), n]).then_inc(s_k[c], 16)
                for r in range(3):
                    rows = slice(r * HD, (r + 1) * HD)
                    if "q" in what:
                        sp.dma_start(qs[rows, c, :, :].bitcast(F32), d["q"][b, g, int(r == 1), :, n]
                                     .rearrange("(h p) n -> p h n", p=HD)).then_inc(s_q[c], 16)

            def for_maxima(b, g):
                for c in range(QB):
                    stacks(q_m, k_m, s_qm, s_km, b, g, c, "kq")

            def rows(c):
                part = slice(c * 4 * HPG, (c + 1) * 4 * HPG)
                for r, src in ((QROWS, rows_hi), (QROWS + 1, rows_lo)):
                    sp.dma_start(q_e[r:r + 1, c, :, :].bitcast(F32), src[part, :].bitcast(F32)).then_inc(s_row[c], 16)

            def store(it, b, g, qb):
                sp.wait_ge(s_norm, it * QB + (qb + 3))
                sp.dma_start(d["ctx"][b, g, :, bass.ts(qb, BLK)], out[qb % 2][:, :]).then_inc(s_st[qb % 2], 16)

            def iteration(it, b, g, nb, ng, last):
                def store_last(qb):
                    if last is not None:
                        store(it - 1, *last, qb)

                for c in range(QB - 1):
                    sp.wait_ge(s_score, it * NS * HPG + ENDS[c] * HPG)
                    stacks(q_e, k_e, s_qe, s_ke, b, g, c, "q")
                    if c > 0:
                        store_last(c - 1)

                def keys(c):
                    sp.wait_ge(s_score, it * NS * HPG + (ENDS[2] + 4 * (c + 1)) * HPG)
                    stacks(q_e, k_e, s_qe, s_ke, b, g, c, "k")
                    sp.wait_ge(s_ctx, it * NS + (ENDS[2] + 4 * (c + 1)))
                    sp.dma_start(v_e[:, 4 * c:4 * c + 4, :], d["v"][bass.ds(b * N + c * BLK, BLK), bass.ds(g * HD, HD)]
                                 .rearrange("(t p) n -> p t n", p=P)).then_inc(s_ve[c], 16)

                keys(0)
                keys(1)
                store_last(2)
                sp.wait_ge(s_unit, it * NU + NU)
                if nb is not None:
                    for_maxima(nb, ng)
                sp.wait_ge(s_rhi, it + 1)
                sp.wait_ge(s_rlo, it + 1)
                for c in range(QB - 1):
                    rows(c)
                keys(2)
                keys(3)
                stacks(q_e, k_e, s_qe, s_ke, b, g, QB - 1, "q")
                rows(QB - 1)
                store_last(QB - 1)

            for_maxima(0, 0)
            for e in range(RING):
                for c in range(DC):
                    sp.dma_start(probs[e][:, c, :], mu[bass.ts(c, P), bass.ts(e, EQ), :].rearrange("p e s -> p (e s)")).then_inc(s_nin, 16)
            iteration(0, 0, 0, 0, 1, None)
            with sp.Fori(1, ITERS - 1) as it:
                iteration(it, it // GROUPS, it % GROUPS, (it + 1) // GROUPS, (it + 1) % GROUPS,
                          ((it - 1) // GROUPS, (it - 1) % GROUPS))
            iteration(ITERS - 1, B - 1, GROUPS - 1, None, None, (B - 1, GROUPS - 2))
            for qb in range(QB):
                store(ITERS - 1, B - 1, GROUPS - 1, qb)
            sp.wait_ge(s_nout, 16)
            for r in range(2):
                sp.wait_ge(s_st[r], 16 + 16 * ITERS * QB // 2)

        @block.gpsimd
        def _(pool):
            pool.memset(ident[:, :], 0.0).then_inc(s_const0, 1)
            pool.memset(ident_b[:, :], 0.0).then_inc(s_const0, 1)
            pool.memset(mask_kq[:, :], 0.0).then_inc(s_const0, 1)
            pool.memset(mask_qk[:, :], 0.0).then_inc(s_const0, 1)
            pool.memset(ones[:, :], 1.0).then_inc(s_const, 1)
            pool.wait_ge(s_const0, 4)
            for m in (ident, ident_b):
                pool.affine_select(out=m[:, :], in_=m[:, :], compare_op=ALU.not_equal, fill=1.0,
                                   base=0, pattern=[[-1, P]], channel_multiplier=1).then_inc(s_const, 1)
            pool.affine_select(out=mask_kq[:, :], in_=mask_kq[:, :], compare_op=ALU.is_ge, fill=MASKED,
                               base=0, pattern=[[1, P]], channel_multiplier=-1).then_inc(s_const, 1)
            pool.affine_select(out=mask_qk[:, :], in_=mask_qk[:, :], compare_op=ALU.is_ge, fill=MASKED,
                               base=0, pattern=[[-1, P]], channel_multiplier=1).then_inc(s_const, 1)
            for e in range(RING):
                pool.wait_ge(s_nsq, e + 1)
                pool.tensor_tensor(probs[e][:, 0:2, :], probs[e][:, 0:2, :], probs[e][:, 2:4, :], ALU.add).then_inc(s_nadd, 1)
                pool.wait_ge(s_nadd, 2 * e + 1)
                pool.tensor_tensor(probs[e][:, 0, :], probs[e][:, 0, :], probs[e][:, 1, :], ALU.add).then_inc(s_nadd, 1)
            pool.sem_inc(s_sum, 2)
            with pool.Fori(0, ITERS) as it:
                for qb in range(1, QB):
                    a = added[qb % 2]
                    pool.wait_ge(s_sum, it * (QB - 1) + {1: 2, 2: 1, 3: 3}[qb])
                    for n, kt in enumerate(ADDED[qb]):
                        if n == 0:
                            continue
                        done = (ENDS[qb - 1] + kt + 1) * HPG
                        pool.wait_ge(s_exp, it * NS * HPG + (ST_BANKS + done))
                        if n > 1:
                            pool.wait_ge(s_add, it * NADD + (adds_before(qb, kt) - 1))
                        first = probs[(ENDS[qb - 1] + ADDED[qb][0]) % RING] if n == 1 else a
                        pool.tensor_tensor(a[:, :, :], first[:, :, :], probs[(ENDS[qb - 1] + kt) % RING][:, :, :],
                                           ALU.add).then_inc(s_add, 1)

        @block.tensor
        def _(pe):
            def unit(it, u):
                qt, h, c = UNITS[u]
                bank, w = ps_m[:, u % M_BANKS, :], min(BLK, (qt + 1) * P - c * BLK)
                if h == 0 and c == 0 and qt % 4 == 0:
                    pe.wait_ge(s_qm[qt // 4], it * 48 + 48)
                    pe.wait_ge(s_km[qt // 4], it * 48 + 48)
                pe.wait_ge(s_taken, it * UF + max(u + 1, M_BANKS))
                last_c = c == qt // 4
                mm = pe.matmul(bank[:, 0:w], q_m[:, qt // 4, h, bass.ts(qt % 4, P)], k_m[:, c * BLK:c * BLK + w],
                               start=True, stop=not last_c)
                if last_c:
                    mm = pe.matmul(bank[:, w - P:w], ident_b[:, :], mask_qk[:, :], start=False, stop=True)
                mm.then_inc(s_unit, 1)

            def rows(it):
                pe.wait_ge(s_neg, it + 1)
                pe.transpose(ps_m[:, 0, 0:P], neg_max[:, :], ident[:, :]).then_inc(s_rt, 1)

            def scores(it, s, h):
                qb, kt = STEPS[s]
                q0 = max(0, kt * P - qb * BLK)
                diagonal = kt >= 4 * qb
                if h == 0 and kt == 0:
                    pe.wait_ge(s_qe[qb], it * 48 + 48)
                    pe.wait_ge(s_row[qb], it * 32 + 64)
                if h == 0 and diagonal and kt % 4 == 0:
                    pe.wait_ge(s_ke[qb], it * 48 + 48)
                pe.wait_ge(s_exp, it * NS * HPG + (s * HPG + h + 1))
                bank = ps_s[:, (s * HPG + h) % ST_BANKS, :]
                mm = pe.matmul(bank[:, q0:BLK], k_e[:, bass.ts(kt, P)], q_e[:, qb, h, q0:BLK],
                               start=True, stop=not diagonal)
                if diagonal:
                    mm = pe.matmul(bank[:, q0:q0 + P], ident_b[:, :], mask_kq[:, :], start=False, stop=True)
                mm.then_inc(s_score, 1)

            def context(it, s):
                qb, kt = STEPS[s]
                q0 = max(0, kt * P - qb * BLK)
                direct, last = kt not in ADDED[qb], kt == 4 * qb + 3
                pe.wait_ge(s_exp, it * NS * HPG + (ST_BANKS + (s + 1) * HPG))
                if kt == 0:
                    pe.wait_ge(s_take, it * 2 * QB + 2 * (qb + 1))
                if kt == 4 * qb:
                    pe.wait_ge(s_ve[qb], it * 16 + 16)
                for h in range(HPG):
                    rows = slice(h * HD, (h + 1) * HD)
                    mm = pe.matmul(ps_c[rows, 0, q0:BLK], v_e[:, kt, :], probs[s % RING][:, h, q0:BLK],
                                   start=kt == 0, stop=last)
                if direct:
                    for h in range(HPG):
                        rows = slice(h * HD, (h + 1) * HD)
                        mm = pe.matmul(ps_d[rows, 0, q0:BLK], ones[:, :], probs[s % RING][:, h, q0:BLK],
                                       start=kt == 0, stop=last and not ADDS[qb])
                mm.then_inc(s_ctx, 1)

            def block_sums(it, qb):
                if ADDS[qb]:
                    pe.wait_ge(s_add, it * NADD + sum(ADDS[:qb + 1]))
                    for h in range(HPG):
                        rows = slice(h * HD, (h + 1) * HD)
                        mm = pe.matmul(ps_d[rows, 0, :], ones[:, :], added[qb % 2][:, h, :], start=False, stop=True)
                    mm.then_inc(s_sum, 1)

            def walk(it, maxima):
                for what, a, h in order(maxima):
                    if what == "maximum":
                        unit(it + 1, a)
                    elif what == "rows":
                        rows(it + 1)
                    elif it is None:
                        continue
                    elif what == "scores":
                        scores(it, a, h)
                    elif what == "context":
                        context(it, a)
                    elif what == "sums":
                        block_sums(it, a)

            pe.sem_inc(s_score, NS * HPG)
            pe.sem_inc(s_ctx, NS)
            pe.wait_ge(s_const, 5)
            pe.wait_ge(s_one, 3)
            def slot_length(e):
                pe.matmul(ps_c[:, 0, e:e + 1], probs[e // EQ][:, 0, bass.ts(e % EQ, S)], ones[:, 0:1],
                          start=True, stop=True).then_inc(s_nsum, 1)

            for u in range(NU):
                if u == NU // 2:
                    pe.wait_ge(s_nadd, 2 * RING)
                if u >= NU // 2 and u % 4 == 0 and (u - NU // 2) // 4 < E:
                    slot_length((u - NU // 2) // 4)
                unit(0, u)
            rows(0)
            with pe.Fori(0, ITERS - 1) as it:
                walk(it, True)
            walk(ITERS - 1, False)

        @block.scalar
        def _(act):
            def exp(it, s, h):
                qb, kt = STEPS[s]
                q0 = max(0, kt * P - qb * BLK)
                act.wait_ge(s_score, (it + 1) * NS * HPG + (s * HPG + h + 1))
                if h == 0:
                    act.wait_ge(s_ctx, it * NS + (NS + s + 1 - RING))
                    if s >= RING:
                        qb0, kt0 = STEPS[s - RING]
                        if kt0 in ADDED[qb0]:
                            act.wait_ge(s_add, it * NADD + adds_before(qb0, kt0))
                act.activation(probs[s % RING][:, h, q0:BLK], ps_s[:, (s * HPG + h) % ST_BANKS, q0:BLK], ACT.Exp).then_inc(s_exp, 1)

            def take(it, qb):
                if ADDS[qb]:
                    act.wait_ge(s_sum, it * (QB - 1) + (2 + qb))
                else:
                    act.wait_ge(s_ctx, it * NS + (NS + ENDS[qb]))
                act.wait_ge(s_norm, it * QB + (qb + 1))
                act.activation(raw[qb % 2][:, :], ps_c[:, 0, :], ACT.Copy).then_inc(s_take, 1)
                act.activation(sums[qb % 2][:, :], ps_d[:, 0, :], ACT.Copy).then_inc(s_take, 1)

            def walk(it, maxima):
                for what, a, h in order(maxima):
                    if what == "scores":
                        exp(it, a, h)
                    elif what == "take":
                        take(it, a)

            act.sem_inc(s_exp, ST_BANKS)
            act.sem_inc(s_take, 2)
            act.wait_ge(s_nin, 16 * RING * DC)
            for e in range(RING):
                act.activation(probs[e][:, :, :], probs[e][:, :, :], ACT.Square).then_inc(s_nsq, 1)
            act.wait_ge(s_nsum, E)
            act.activation(n_len[:, :], ps_c[:, 0, 0:E], ACT.Sqrt).then_inc(s_nlen, 1)
            act.wait_ge(s_ninv, 2)
            act.dma_start(d["inv"], n_inv[:, :]).then_inc(s_nout, 16)
            with act.Fori(0, ITERS - 1) as it:
                walk(it, True)
            walk(ITERS - 1, False)

        @block.vector
        def _(dve):
            def maximum(it, u):
                qt, h, c = UNITS[u]
                w, at = min(BLK, (qt + 1) * P - c * BLK), (qt // 4 * HPG + h) * 4 + qt % 4
                dve.wait_ge(s_unit, it * NU + (u + 1))
                dve.tensor_reduce(parts[:, at, c:c + 1], ps_m[:, u % M_BANKS, 0:w], AX.X, ALU.max).then_inc(s_taken, 1)

            def rows(it):
                dve.wait_ge(s_taken, it * UF + (M_BANKS + NU))
                dve.tensor_reduce(neg_max[:, 0:QB * HPG * 4], parts[:, :, :], AX.X, ALU.max, negate=True).then_inc(s_neg, 1)
                dve.wait_ge(s_rt, it + 1)
                for c in range(QB):
                    dve.wait_ge(s_row[c], it * 32 + 32)
                row = ps_m[0:QB * HPG * 4, 0, 0:P]
                dve.tensor_copy(rows_hi[:, :], row).then_inc(s_rhi, 1)
                dve.wait_ge(s_rhi, it + 1)
                dve.tensor_tensor(rows_lo[:, :], row, rows_hi[:, :], ALU.subtract).then_inc(s_rlo, 1)
                dve.wait_ge(s_rlo, it + 1)
                dve.sem_inc(s_taken, 1)

            def inverse(it, qb, k):
                if k == 0:
                    dve.wait_ge(s_norm, it * QB + (qb + 2))
                    dve.wait_ge(s_take, it * 2 * QB + (2 + 2 * (qb + 1)))
                dve.reciprocal(inv[:, bass.ts(k, P)], sums[qb % 2][:, bass.ts(k, P)]).then_inc(s_inv, 1)

            def normalise(it, qb):
                n, r = it * QB + qb, qb % 2
                dve.wait_ge(s_inv, n * 4 + 4)
                dve.wait_ge(s_st[r], it * 32 + 16 * (qb // 2 + 1))
                dve.tensor_tensor(out[r][:, :], raw[r][:, :], inv[:, :], ALU.mult).then_inc(s_norm, 1)

            def walk(it, maxima):
                for what, a, h in order(maxima):
                    if what == "maximum":
                        maximum(it + 1, a)
                    elif what == "rows":
                        rows(it + 1)
                    elif what == "inverse":
                        inverse(it, a, h)
                    elif what == "normalise":
                        normalise(it, a)

            dve.sem_inc(s_taken, M_BANKS)
            dve.sem_inc(s_norm, 2)
            for sm in s_row:
                dve.sem_inc(sm, 32)
            for sm in s_st:
                dve.sem_inc(sm, 16)
            dve.memset(parts[:, :, :], -3.0e38).then_inc(s_one, 1)
            dve.memset(neg_max[:, :], 0.0).then_inc(s_one, 1)
            dve.memset(k_e[QROWS:MROWS, :].bitcast(F32), 1.0).then_inc(s_one, 1)
            dve.wait_ge(s_one, 3)
            for u in range(NU):
                if u == NU - 8:
                    dve.wait_ge(s_nlen, 1)
                    dve.tensor_scalar_max(n_max[:, :], n_len[:, :], L2_EPS).then_inc(s_ninv, 1)
                    dve.wait_ge(s_ninv, 1)
                    dve.reciprocal(n_inv[:, :], n_max[:, :]).then_inc(s_ninv, 1)
                maximum(0, u)
            rows(0)
            with dve.Fori(0, ITERS - 1) as it:
                walk(it, True)
            walk(ITERS - 1, False)


def skewed(eng, parts, tiles, unroll=4):
    most = max(lag for lag, _ in parts)
    peeled = max(-(-most // unroll), 1)
    for k in range(peeled * unroll):
        for lag, part in parts:
            if k >= lag:
                part(k - lag, (k - lag) % unroll, (k - lag) // unroll)
    with eng.Fori(peeled, tiles // unroll) as i:
        for t in range(unroll):
            for lag, part in parts:
                part(i * unroll + (t - lag), (t - lag) % unroll, i + (t - lag) // unroll)
    for k in range(tiles, tiles + most):
        for lag, part in parts:
            if k - lag < tiles:
                part(k - lag, (k - lag) % unroll, (k - lag) // unroll)


R4 = 4
TT_ALL = TOK // P


def post(nc, sems, x, Wo, bo, gamma, beta, scale, d):
    with ExitStack() as ctx:
        al = Names(nc, ctx, sems)
        ring = lambda name, shape, dt=F32: [al.sbuf(f"p3_{name}{r}", shape, dt) for r in range(R4)]
        sem = lambda name: al.sem("p3_" + name)
        sem4 = lambda name: [al.sem(f"p3_{name}{r}") for r in range(R4)]
        ident = al.sbuf("p3_ident", [P, P])
        w_raw = al.sbuf("p3_w", [P, GROUPS, D])
        w_hi, w_lo = al.sbuf("p3_w_hi", [P, GROUPS, D], F32R), al.sbuf("p3_w_lo", [P, GROUPS, D], F32R)
        bo_r, gamma_r, beta_r = (al.sbuf(f"p3_{n}", [P, D]) for n in ("bo", "gamma", "beta"))
        scale_r = al.sbuf("p3_scale", [P, 1])
        c_raw, c_hi, c_lo = ring("c", [P, GROUPS, P]), ring("c_hi", [P, GROUPS, P], F32R), ring("c_lo", [P, GROUPS, P], F32R)
        x_in, x_b, y, x1 = ring("x", [P, D]), ring("xb", [P, D]), ring("y", [P, D]), ring("x1", [P, D])
        z, zg, xl, sq, xn = (ring(n, [P, D]) for n in ("z", "zg", "xl", "sq", "xn"))
        xt = ring("xt", [P, DC, P])
        n1, n2 = ring("n1", [P, 12]), ring("n2", [P, 12])
        l2 = ring("l2", [P, 5])
        ps_p, ps_t = al.psum("p3_ps_p", R4), al.psum("p3_ps_t", R4)

        s_id0, s_id, s_w, s_vec, s_whi, s_wlo = (sem(n) for n in ("id0", "id", "w", "vec", "w_hi", "w_lo"))
        s_c, s_x, s_chi, s_clo = sem4("c_in"), sem4("x_in"), sem("c_hi"), sem("c_lo")
        s_proj, s_xb, s_y, s_n1, s_d1, s_x1 = (sem(n) for n in ("proj", "xb", "y", "inv1", "dev1", "x1"))
        s_y2, s_n2, s_d2, s_z, s_g = (sem(n) for n in ("stats2", "inv2", "dev2", "z", "xl"))
        s_sq, s_nrm, s_inv, s_xn = (sem(n) for n in ("sumsq", "norm", "inv", "xn"))
        s_tr, s_xt = sem("transposed"), sem("xt")
        o_x1, o_xl, o_t = sem4("x1_out"), sem4("xl_out"), sem4("t_out")

        block = ctx.enter_context(nc.Block())
        x_d = x.rearrange("b n c -> (b n) c")

        @block.sync
        def _(sp):
            sp.dma_start(w_raw[:, :, :], Wo.rearrange("(g p) n -> p g n", p=P)).then_inc(s_w, 16)
            for dst, src in ((bo_r, bo), (gamma_r, gamma), (beta_r, beta), (scale_r, scale)):
                sp.dma_start(dst[:, :], src.partition_broadcast(P)).then_inc(s_vec, 16)

            def load(n, r, u):
                b, m = n // NT, n % NT
                sp.wait_ge(s_clo, n + 1)
                sp.dma_start(c_raw[r][:, :, :], d["ctx"][b, :, :, bass.ds(m * P, P)].rearrange("g p n -> p g n")).then_inc(s_c[r], 16)
                sp.wait_ge(s_xb, n + 1)
                sp.dma_start(x_in[r][:, :], x_d[bass.ds(n * P, P), :]).then_inc(s_x[r], 16)

            def store_x1(n, r, u):
                sp.wait_ge(s_x1, n + 1 + R4)
                sp.dma_start(d["x1"][bass.ds(n * P, P), :], x1[r][:, :]).then_inc(o_x1[r], 16)

            def store_xl(n, r, u):
                sp.wait_ge(s_g, n * 2 + (2 + 2 * R4))
                sp.dma_start(d["xl"][n, :, :], xl[r][:, :]).then_inc(o_xl[r], 16)

            def store_t(n, r, u):
                sp.wait_ge(s_xt, n + 1 + R4)
                sp.dma_start(d["xT"][n, :, :, :], xt[r][:, :, :]).then_inc(o_t[r], 16)

            skewed(sp, [(0, load), (6, store_x1), (10, store_xl), (14, store_t)], TT_ALL)
            for r in range(R4):
                sp.wait_ge(o_x1[r], 16 * (1 + TT_ALL // R4))
                sp.wait_ge(o_xl[r], 16 * (1 + TT_ALL // R4))
                sp.wait_ge(o_t[r], 16 * (1 + TT_ALL // R4))

        @block.gpsimd
        def _(pool):
            pool.memset(ident[:, :], 0.0).then_inc(s_id0, 1)
            pool.wait_ge(s_id0, 1)
            pool.affine_select(out=ident[:, :], in_=ident[:, :], compare_op=ALU.not_equal, fill=1.0,
                               base=0, pattern=[[-1, P]], channel_multiplier=1).then_inc(s_id, 1)
            pool.wait_ge(s_vec, 64)

            def add_bias(n, r, u):
                pool.wait_ge(s_x[r], u * 16 + 16)
                pool.wait_ge(s_y, n * 1 + 1)
                pool.tensor_tensor(x_b[r][:, :], x_in[r][:, :], bo_r[:, :], ALU.add).then_inc(s_xb, 1)

            def affine(n, r, u):
                pool.wait_ge(s_z, n + 1 + R4)
                pool.tensor_tensor(zg[r][:, :], z[r][:, :], gamma_r[:, :], ALU.mult).then_inc(s_g, 1)
                pool.wait_ge(s_g, n * 2 + (1 + 2 * R4))
                pool.wait_ge(s_xn, n + 1)
                pool.wait_ge(o_xl[r], u * 16 + 16)
                pool.tensor_tensor(xl[r][:, :], zg[r][:, :], beta_r[:, :], ALU.add).then_inc(s_g, 1)

            skewed(pool, [(0, add_bias), (6, affine)], TT_ALL)

        @block.tensor
        def _(pe):
            pe.sem_inc(s_proj, R4)
            pe.sem_inc(s_tr, R4)
            pe.wait_ge(s_wlo, 1)
            pe.wait_ge(s_id, 1)

            def project(n, r, u):
                pe.wait_ge(s_clo, n + 1 + R4)
                pe.wait_ge(s_y, n + 1)
                for g in range(GROUPS):
                    mm = three_passes(pe, ps_p[:, r, :], c_hi[r][:, g, :], c_lo[r][:, g, :],
                                      w_hi[:, g, :], w_lo[:, g, :], g == 0, g == GROUPS - 1)
                mm.then_inc(s_proj, 1)

            def transpose(n, r, u):
                pe.wait_ge(s_xn, n + 1 + R4)
                pe.wait_ge(s_xt, n + 1)
                for c in range(DC):
                    mm = pe.transpose(ps_t[:, r, bass.ts(c, P)], xn[r][:, bass.ts(c, P)], ident[:, :])
                mm.then_inc(s_tr, 1)

            skewed(pe, [(0, project), (10, transpose)], TT_ALL)

        @block.scalar
        def _(act):
            for s in (s_x1, s_z, s_xn, s_xt):
                act.sem_inc(s, R4)

            def context_hi(n, r, u):
                act.wait_ge(s_c[r], u * 16 + 16)
                act.wait_ge(s_proj, n + 1)
                act.activation(c_hi[r][:, :, :], c_raw[r][:, :, :], ACT.Copy).then_inc(s_chi, 1)

            def dev1(n, r, u):
                act.wait_ge(s_y, n + 1 + R4)
                act.wait_ge(s_n1, n * 2 + 2)
                act.activation(n1[r][:, 9:10], n1[r][:, 8:9], ACT.Sqrt).then_inc(s_d1, 1)

            def norm1(n, r, u):
                act.wait_ge(s_n1, n * 2 + (2 + 2 * R4))
                act.wait_ge(o_x1[r], u * 16 + 16)
                act.wait_ge(s_z, n + 1)
                act.activation(x1[r][:, :], y[r][:, :], ACT.Identity, scale=n1[r][:, 10:11], bias=n1[r][:, 11:12]).then_inc(s_x1, 1)

            def dev2(n, r, u):
                act.wait_ge(s_y2, n + 1)
                act.wait_ge(s_n2, n * 2 + 2)
                act.activation(n2[r][:, 9:10], n2[r][:, 8:9], ACT.Sqrt).then_inc(s_d2, 1)

            def norm2(n, r, u):
                act.wait_ge(s_n2, n * 2 + (2 + 2 * R4))
                act.wait_ge(s_g, n * 2 + 2)
                act.activation(z[r][:, :], x1[r][:, :], ACT.Identity, scale=n2[r][:, 10:11], bias=n2[r][:, 11:12]).then_inc(s_z, 1)

            def squares(n, r, u):
                act.wait_ge(s_g, n * 2 + (2 + 2 * R4))
                act.wait_ge(s_inv, n * 3 + 3)
                act.activation(sq[r][:, :], xl[r][:, :], ACT.Square, accum_out=l2[r][:, 0:1]).then_inc(s_sq, 1)
                act.wait_ge(s_sq, n + 1)
                act.activation(l2[r][:, 1:2], l2[r][:, 0:1], ACT.Sqrt).then_inc(s_nrm, 1)

            def unit_rows(n, r, u):
                act.wait_ge(s_inv, n * 3 + (3 + 3 * R4))
                act.wait_ge(s_tr, n + 1)
                act.activation(xn[r][:, :], xl[r][:, :], ACT.Copy, scale=l2[r][:, 4:5]).then_inc(s_xn, 1)

            def copy(n, r, u):
                act.wait_ge(s_tr, n + 1 + R4)
                act.wait_ge(o_t[r], u * 16 + 16)
                act.activation(xt[r][:, :, :], ps_t[:, r, :], ACT.Copy).then_inc(s_xt, 1)

            skewed(act, [(0, context_hi), (12, copy), (10, unit_rows), (8, squares), (6, norm2), (5, dev2), (3, norm1), (2, dev1)], TT_ALL)

        @block.vector
        def _(dve):
            dve.wait_ge(s_w, 16)
            dve.tensor_copy(w_hi[:, :, :], w_raw[:, :, :]).then_inc(s_whi, 1)
            dve.wait_ge(s_whi, 1)
            dve.tensor_tensor(w_lo[:, :, :], w_raw[:, :, :], w_hi[:, :, :], ALU.subtract).then_inc(s_wlo, 1)
            dve.wait_ge(s_vec, 64)
            dve.sem_inc(s_y, R4)
            dve.sem_inc(s_n1, 2 * R4)
            dve.sem_inc(s_n2, 2 * R4)
            dve.sem_inc(s_inv, 3 * R4)
            dve.sem_inc(s_xb, R4)
            dve.sem_inc(s_clo, R4)
            dve.sem_inc(s_g, 2 * R4)
            for r in range(R4):
                dve.sem_inc(o_x1[r], 16)
                dve.sem_inc(o_xl[r], 16)
                dve.sem_inc(o_t[r], 16)
            steps = {k: al.sem(f"p3_dve_{k}") for k in ("a", "b", "c", "d")}

            def statistics(n, small, rows, s, out_sem):
                dve.bn_stats(small[:, 0:6], rows).then_inc(s, 1)
                dve.wait_ge(s, n * 3 + 1)
                dve.memset(small[:, 8:9], LN_EPS).then_inc(s, 1)
                dve.bn_aggr(small[:, 6:8], small[:, 0:6]).then_inc(s, 1)
                dve.wait_ge(s, n * 3 + 3)
                dve.tensor_tensor(small[:, 8:9], small[:, 7:8], small[:, 8:9], ALU.add).then_inc(out_sem, 1)

            def context_lo(n, r, u):
                dve.wait_ge(s_chi, n + 1)
                dve.tensor_tensor(c_lo[r][:, :, :], c_raw[r][:, :, :], c_hi[r][:, :, :], ALU.subtract).then_inc(s_clo, 1)

            def first(n, r, u):
                dve.wait_ge(s_proj, n + 1 + R4)
                dve.wait_ge(s_xb, n + 1 + R4)
                dve.wait_ge(s_x1, n + 1)
                dve.tensor_tensor(y[r][:, :], ps_p[:, r, :], x_b[r][:, :], ALU.add).then_inc(steps["a"], 1)
                dve.wait_ge(steps["a"], n + 1)
                statistics(n, n1[r], y[r][:, :], steps["b"], s_y)

            def inverse(n, small, s_dev, s_inv_):
                dve.wait_ge(s_dev, n + 1)
                dve.reciprocal(small[:, 10:11], small[:, 9:10]).then_inc(s_inv_, 1)
                dve.wait_ge(s_inv_, n * 2 + (1 + 2 * R4))
                dve.tensor_scalar(small[:, 11:12], small[:, 6:7], small[:, 10:11], -1.0, ALU.mult, ALU.mult).then_inc(s_inv_, 1)

            def inverse1(n, r, u):
                inverse(n, n1[r], s_d1, s_n1)

            def second(n, r, u):
                dve.wait_ge(s_x1, n + 1 + R4)
                statistics(n, n2[r], x1[r][:, :], steps["c"], s_y2)

            def inverse2(n, r, u):
                inverse(n, n2[r], s_d2, s_n2)

            def unit(n, r, u):
                dve.wait_ge(s_nrm, n + 1)
                dve.tensor_scalar_max(l2[r][:, 2:3], l2[r][:, 1:2], L2_EPS).then_inc(s_inv, 1)
                dve.wait_ge(s_inv, n * 3 + (1 + 3 * R4))
                dve.reciprocal(l2[r][:, 3:4], l2[r][:, 2:3]).then_inc(s_inv, 1)
                dve.wait_ge(s_inv, n * 3 + (2 + 3 * R4))
                dve.tensor_tensor(l2[r][:, 4:5], l2[r][:, 3:4], scale_r[:, :], ALU.mult).then_inc(s_inv, 1)

            skewed(dve, [(0, context_lo), (9, unit), (6, inverse2), (4, second), (3, inverse1), (1, first)], TT_ALL)


JG = 4
STAGE = 4
TG = NT // JG


def slots(nc, sems, mu, W1, b1_t, W2, b2, d):
    with ExitStack() as ctx:
        al = Names(nc, ctx, sems)
        sem = lambda name: al.sem("p4_" + name)
        pair = lambda name, shape: (al.sbuf(f"p4_{name}_lo", shape, F32R), al.sbuf(f"p4_{name}_hi", shape, F32R))
        xT_lo, xT_hi = pair("xT", [P, NT, DC, P])
        xl_lo, xl_hi = pair("xl", [P, NT, D])
        m_lo, m_hi = zip(*(pair(f"mu{r}", [P, DC, S]) for r in range(2)))
        w1_lo, w1_hi = pair("w1", [P, DC, H])
        w2_lo, w2_hi = pair("w2", [P, D])
        b1_c, inv_n = al.sbuf("p4_b1", [P, E]), al.sbuf("p4_inv_n", [P, E])
        m_raw, w1_raw, w2_raw = (al.sbuf(f"p4_{n}_raw", [P, D]) for n in ("mu", "w1", "w2"))
        own, own_b1 = [al.sbuf(f"p4_own{r}", [P, 1]) for r in range(2)], al.sbuf("p4_own_b1", [P, 1])
        b2_r = al.sbuf("p4_b2", [P, D])
        ident = al.sbuf("p4_ident", [P, P])
        logit = al.sbuf("p4_logit", [P, JG, BANK])
        ex = [al.sbuf(f"p4_ex{r}", [P, JG, BANK]) for r in range(2)]
        most = al.sbuf("p4_most", [P, JG, BANK])
        col = [al.sbuf(f"p4_col{r}", [P, 12]) for r in range(2)]
        eT_hi = [al.sbuf(f"p4_eT_hi{r}", [P, TG, S], F32R) for r in range(2)]
        eT_lo = [al.sbuf(f"p4_eT_lo{r}", [P, TG, S], F32R) for r in range(2)]
        si = al.sbuf("p4_si", [P, D])
        siT_hi, siT_lo = al.sbuf("p4_siT_hi", [P, DC, S], F32R), al.sbuf("p4_siT_lo", [P, DC, S], F32R)
        h = al.sbuf("p4_h", [P, S])
        h_hi, h_lo = al.sbuf("p4_h_hi", [P, S], F32R), al.sbuf("p4_h_lo", [P, S], F32R)
        so = si
        so_hi, so_lo = al.sbuf("p4_so_hi", [P, D], F32R), al.sbuf("p4_so_lo", [P, D], F32R)
        m_col, m_row = al.sbuf("p4_m_col", [P, P]), al.sbuf("p4_m_row", [NT, P])
        ps_l, ps_t, ps_s, ps_e = al.psum("p4_ps_l", JG), al.psum("p4_ps_t", 2), al.psum("p4_ps_s", 1), al.psum("p4_ps_e", 1)

        s_xT, s_xl = [sem(f"xT{j}") for j in range(STAGE)], [sem(f"xl{j}") for j in range(STAGE)]
        s_xThi, s_xTlo, s_xlhi, s_xllo = sem("xT_hi"), sem("xT_lo"), sem("xl_hi"), sem("xl_lo")
        s_mu, s_w, s_b2, s_vec = sem("mu"), sem("weights"), sem("b2"), sem("vectors")
        s_muhi, s_mulo, s_whi, s_wlo = sem("mu_hi"), sem("mu_lo"), sem("w_hi"), sem("w_lo")
        s_id0, s_id, s_reset, s_own = sem("id0"), sem("id"), sem("reset"), sem("own")
        s_log, s_cp, s_most, s_ex, s_max, s_neg = (sem(n) for n in ("logits", "copied", "most", "exp", "max", "negated"))
        s_sum, s_rs, s_tr, s_ehi, s_elo, s_prod = (sem(n) for n in ("sum", "inverse", "transposed", "e_hi", "e_lo", "product"))
        s_si, s_sT, s_sThi, s_sTlo = sem("slot_in"), sem("slot_in_t"), sem("slot_in_hi"), sem("slot_in_lo")
        s_h, s_g, s_hhi, s_hlo, s_o = sem("hidden"), sem("gelu"), sem("h_hi"), sem("h_lo"), sem("slot_out")
        s_add, s_ohi, s_olo = sem("biased"), sem("o_hi"), sem("o_lo")
        s_mt, s_mc, s_mr, s_mrow = sem("most_t"), sem("m_col"), sem("m_row_t"), sem("m_row")
        o_l, o_so, o_m = sem("logits_stored"), sem("slot_out_stored"), sem("maxima_stored")
        block = ctx.enter_context(nc.Block())
        U = 2
        mu_e = mu.rearrange("(c p) e s -> p e c s", p=P)
        w1_e = W1.rearrange("e (c p) h -> p e c h", p=P)
        group = lambda j: slice(j * TG, (j + 1) * TG)

        @block.sync
        def _(sp):
            sp.dma_start(b1_c[:, :], b1_t).then_inc(s_vec, 16)
            sp.dma_start(inv_n[:, :], d["inv"]).then_inc(s_vec, 16)

            with sp.Fori(0, B) as b:
                def load_mu(n, r, u):
                    g = b * E + n
                    sp.wait_ge(s_mulo, g + 1)
                    for c in range(DC):
                        sp.dma_start(m_raw[:, bass.ts(c, S)], mu_e[:, bass.ds(n, 1), c, :]
                                     .rearrange("p e s -> p (e s)")).then_inc(s_mu, 16)

                def store_logits(n, r, u):
                    g = b * E + n
                    sp.wait_ge(s_cp, g * JG + 2 * JG)
                    sp.dma_start(d["logit"][g], logit[:, :, :]).then_inc(o_l, 16)

                def load_weights(n, r, u):
                    g = b * E + n
                    sp.wait_ge(s_wlo, g * 2 + 2)
                    for c in range(DC):
                        sp.dma_start(w1_raw[:, bass.ts(c, H)], w1_e[:, bass.ds(n, 1), c, :]
                                     .rearrange("p e h -> p (e h)")).then_inc(s_w, 16)
                    sp.dma_start(w2_raw[:, :], W2[n]).then_inc(s_w, 16)
                    sp.wait_ge(s_add, g + 1)
                    sp.dma_start(b2_r[:, :], b2[n].partition_broadcast(P)).then_inc(s_b2, 16)

                def store_out(n, r, u):
                    g = b * E + n
                    sp.wait_ge(s_ohi, g + 1)
                    sp.dma_start(d["so"][b, 0, :, n, :], so_hi[:, :].bitcast(F32)).then_inc(o_so, 16)
                    sp.wait_ge(s_olo, g + 2)
                    sp.dma_start(d["so"][b, 1, :, n, :], so_lo[:, :].bitcast(F32)).then_inc(o_so, 16)

                skewed(sp, [(0, load_mu), (1, store_logits), (2, load_weights), (3, store_out)], E, U)
            sp.wait_ge(o_l, 16 + 16 * B * E)
            sp.wait_ge(o_so, 32 + 32 * B * E)
            sp.wait_ge(o_m, 16 + 16 * B)

        @block.gpsimd
        def _(pool):
            pool.memset(ident[:, :], 0.0).then_inc(s_id0, 1)
            pool.wait_ge(s_id0, 1)
            pool.affine_select(out=ident[:, :], in_=ident[:, :], compare_op=ALU.not_equal, fill=1.0,
                               base=0, pattern=[[-1, P]], channel_multiplier=1).then_inc(s_id, 1)
            for b in range(B):
                pool.wait_ge(s_tr, b * E * JG + JG)
                for t in range(NT):
                    if t >= STAGE:
                        pool.wait_ge(s_xTlo, b * NT + t + 1 - STAGE)
                    pool.dma_start(ex[0][:, t % STAGE, :], d["xT"][b * NT + t].rearrange("p c n -> p (c n)")).then_inc(s_xT[t % STAGE], 16)
                pool.wait_ge(s_mt, b * JG + JG)
                pool.memset(most[:, :, :], -3.0e38).then_inc(s_reset, 1)
                pool.wait_ge(s_tr, b * E * JG + 2 * JG)
                for t in range(NT):
                    if t >= STAGE:
                        pool.wait_ge(s_xllo, b * NT + t + 1 - STAGE)
                    pool.dma_start(ex[1][:, t % STAGE, :], d["xl"][b * NT + t]).then_inc(s_xl[t % STAGE], 16)

        @block.tensor
        def _(pe):
            pe.sem_inc(s_log, 2 * JG)
            pe.sem_inc(s_tr, 2 * JG)
            pe.sem_inc(s_prod, 2)
            pe.sem_inc(s_mt, JG)
            for s in (s_sT, s_h, s_o, s_mr):
                pe.sem_inc(s, 1)
            pe.wait_ge(s_id, 1)
            with pe.Fori(0, B) as b:
                def logits(j):
                    def part(n, r, u):
                        g = b * E + n
                        if j == 0:
                            pe.wait_ge(s_mulo, g + 2)
                        if isinstance(n, int) and n == 0:
                            pe.wait_ge(s_xTlo, b * NT + (j + 1) * TG)
                        pe.wait_ge(s_cp, g * JG + (j + 1))
                        for c in range(DC):
                            mm = three_passes(pe, ps_l[:, j, :], m_hi[r][:, c, :], m_lo[r][:, c, :],
                                              xT_hi[:, group(j), c, :], xT_lo[:, group(j), c, :], c == 0, c == DC - 1)
                        mm.then_inc(s_log, 1)
                    return part

                def transpose(j):
                    def part(n, r, u):
                        g = b * E + n
                        pe.wait_ge(s_ex, g * JG + (j + 1 + JG))
                        pe.wait_ge(s_elo, g * JG + (j + 1))
                        for t in range(TG):
                            mm = pe.transpose(ps_t[:, j % 2, bass.ts(t, P)], ex[r][:, j, bass.ts(t, P)], ident[:, :])
                        mm.then_inc(s_tr, 1)
                    return part

                def product(j):
                    def part(n, r, u):
                        g = b * E + n
                        if isinstance(n, int) and n == 0:
                            pe.wait_ge(s_xllo, b * NT + (j + 1) * TG)
                        if j == 0:
                            pe.wait_ge(s_si, g + 1)
                        pe.wait_ge(s_elo, g * JG + (j + 1 + 2))
                        for t in range(TG):
                            mm = three_passes(pe, ps_s[:, 0, :], eT_hi[j % 2][:, t, :], eT_lo[j % 2][:, t, :],
                                              xl_hi[:, j * TG + t, :], xl_lo[:, j * TG + t, :],
                                              j == 0 and t == 0, j == JG - 1 and t == TG - 1)
                        mm.then_inc(s_prod, 1)
                    return part

                def slot_in_t(n, r, u):
                    g = b * E + n
                    pe.wait_ge(s_si, g + 2)
                    pe.wait_ge(s_add, g + 1)
                    for c in range(DC):
                        mm = pe.transpose(ps_e[:, 0, bass.ts(c, P)], si[:, bass.ts(c, P)], ident[:, :])
                    mm.then_inc(s_sT, 1)

                def hidden(n, r, u):
                    g = b * E + n
                    pe.wait_ge(s_wlo, g * 2 + 3)
                    pe.wait_ge(s_sTlo, g + 1)
                    for c in range(DC):
                        mm = three_passes(pe, ps_e[:, 0, 0:S], w1_hi[:, c, :], w1_lo[:, c, :],
                                          siT_hi[:, c, :], siT_lo[:, c, :], c == 0, c == DC - 1)
                    mm.then_inc(s_h, 1)

                def slot_out(n, r, u):
                    g = b * E + n
                    pe.wait_ge(s_wlo, g * 2 + 4)
                    pe.wait_ge(s_hlo, g + 2)
                    three_passes(pe, ps_e[:, 0, :], h_hi[:, :], h_lo[:, :], w2_hi[:, :], w2_lo[:, :], True, True).then_inc(s_o, 1)

                skewed(pe, [(1, logits(0)), (3, slot_in_t), (1, logits(1)), (1, logits(2)), (3, hidden),
                            (2, transpose(0)), (1, logits(3)), (2, transpose(1)), (3, slot_out), (2, product(0)), (2, transpose(2)),
                            (2, product(1)), (2, transpose(3)), (2, product(2)), (2, product(3))], E, U)
                for j in range(JG):
                    pe.wait_ge(s_most, b * E * JG + (E * JG + j + 1))
                    pe.wait_ge(s_cp, b * E * JG + (E * JG + j + 1))
                    for t in range(TG):
                        mm = pe.transpose(ps_l[:, j, bass.ts(t, P)], most[:, j, bass.ts(t, P)], ident[:, :])
                    mm.then_inc(s_mt, 1)
                pe.wait_ge(s_mc, b * JG + (JG + 1))
                pe.wait_ge(s_add, b * E + E + 1)
                pe.transpose(ps_e[:, 0, 0:P], m_col[:, :], ident[:, :]).then_inc(s_mr, 1)

        @block.scalar
        def _(act):
            act.sem_inc(s_cp, JG)
            act.sem_inc(s_ex, JG)
            act.sem_inc(s_si, 1)
            with act.Fori(0, B) as b:
                def unit_rows_hi(n, r, u):
                    if isinstance(n, int) and n == 0:
                        act.wait_ge(s_log, b * E * JG + 2 * JG)
                        for t in range(NT):
                            act.wait_ge(s_xT[t % STAGE], b * (16 * NT // STAGE) + (t // STAGE * 16 + 16))
                            act.activation(xT_hi[:, t, :, :], ex[0][:, t % STAGE, :], ACT.Copy).then_inc(s_xThi, 1)

                def vectors_hi(n, r, u):
                    g = b * E + n
                    act.wait_ge(s_mu, g * 16 * DC + 16 * DC)
                    act.wait_ge(s_log, g * JG + JG)
                    act.activation(m_hi[r][:, :, :], m_raw[:, :], ACT.Copy).then_inc(s_muhi, 1)

                def rows_hi(n, r, u):
                    if isinstance(n, int) and n == 0:
                        act.wait_ge(s_prod, b * E * JG + 2)
                        for t in range(NT):
                            act.wait_ge(s_xl[t % STAGE], b * (16 * NT // STAGE) + (t // STAGE * 16 + 16))
                            act.activation(xl_hi[:, t, :], ex[1][:, t % STAGE, :], ACT.Copy).then_inc(s_xlhi, 1)

                def copy(j):
                    def part(n, r, u):
                        g = b * E + n
                        act.wait_ge(s_log, g * JG + (j + 1 + 2 * JG))
                        act.wait_ge(s_most, g * JG + (j + 1))
                        act.wait_ge(s_ex, g * JG + (j + 1))
                        act.wait_ge(o_l, g * 16 + 16)
                        act.activation(logit[:, j, :], ps_l[:, j, :], ACT.Copy, scale=own[r][:, 0:1]).then_inc(s_cp, 1)
                    return part

                def exp(j):
                    def part(n, r, u):
                        g = b * E + n
                        act.wait_ge(s_neg, g + 1)
                        act.wait_ge(s_tr, g * JG + (j + 1))
                        if isinstance(n, int) and n == 0:
                            act.wait_ge(s_xTlo, b * NT + NT)
                        if isinstance(n, int) and n == 1:
                            act.wait_ge(s_xllo, b * NT + NT)
                        act.activation(ex[r][:, j, :], logit[:, j, :], ACT.Exp, bias=col[r][:, 5:6],
                                       accum_out=col[r][:, 6 + j:7 + j]).then_inc(s_ex, 1)
                    return part

                def split_hi(j):
                    def part(n, r, u):
                        g = b * E + n
                        act.wait_ge(s_tr, g * JG + (j + 1 + 2 * JG))
                        act.wait_ge(s_prod, g * JG + (j + 1))
                        act.activation(eT_hi[j % 2][:, :, :], ps_t[:, j % 2, :], ACT.Copy).then_inc(s_ehi, 1)
                    return part

                def slot_in(n, r, u):
                    g = b * E + n
                    act.wait_ge(s_prod, g * JG + (JG + 2))
                    act.wait_ge(s_rs, g + 1)
                    act.wait_ge(s_sT, g + 1)
                    act.wait_ge(s_olo, g + 1)
                    act.activation(si[:, :], ps_s[:, 0, :], ACT.Copy, scale=col[r][:, 11:12]).then_inc(s_si, 1)

                def slot_in_hi(n, r, u):
                    g = b * E + n
                    act.wait_ge(s_sT, g + 2)
                    act.wait_ge(s_h, g + 1)
                    act.activation(siT_hi[:, :, :], ps_e[:, 0, :], ACT.Copy).then_inc(s_sThi, 1)

                def gelu(n, r, u):
                    g = b * E + n
                    act.wait_ge(s_h, g + 2)
                    act.wait_ge(s_hlo, g + 1)
                    act.activation(h[:, :], ps_e[:, 0, 0:S], ACT.Gelu, bias=own_b1[:, :]).then_inc(s_g, 1)
                    act.wait_ge(s_g, g + 2)
                    act.wait_ge(s_o, g + 1)
                    act.activation(h_hi[:, :], h[:, :], ACT.Copy).then_inc(s_hhi, 1)

                def out_hi(n, r, u):
                    g = b * E + n
                    act.wait_ge(s_add, g + 2)
                    act.wait_ge(o_so, g * 32 + 32)
                    act.activation(so_hi[:, :], so[:, :], ACT.Copy).then_inc(s_ohi, 1)

                def weights_hi(n, r, u):
                    g = b * E + n
                    act.wait_ge(s_w, g * (16 * (DC + 1)) + 16 * (DC + 1))
                    act.wait_ge(s_h, g + 1)
                    act.activation(w1_hi[:, :, :], w1_raw[:, :], ACT.Copy).then_inc(s_whi, 1)
                    act.wait_ge(s_o, g + 1)
                    act.activation(w2_hi[:, :], w2_raw[:, :], ACT.Copy).then_inc(s_whi, 1)

                skewed(act, [(3, slot_in), (1, copy(0)), (3, slot_in_hi), (1, copy(1)), (1, copy(2)), (3, gelu),
                             (2, split_hi(0)), (1, copy(3)), (2, split_hi(1)), (1, exp(0)), (1, exp(1)), (2, split_hi(2)),
                             (1, exp(2)), (1, exp(3)), (3, out_hi), (2, split_hi(3)), (0, vectors_hi), (0, unit_rows_hi), (1, rows_hi), (2, weights_hi)], E, U)
                act.wait_ge(s_mr, b + 2)
                act.wait_ge(o_m, b * 16 + 16)
                act.activation(m_row[:, :], ps_e[0:NT, 0, 0:P], ACT.Copy).then_inc(s_mrow, 1)
                act.wait_ge(s_mrow, b + 1)
                act.dma_start(d["top"][b], m_row[:, :]).then_inc(o_m, 16)

        @block.vector
        def _(dve):
            dve.sem_inc(s_most, JG)
            for s in (s_elo, s_wlo):
                dve.sem_inc(s, 2)
            for s in (s_mulo, s_olo):
                dve.sem_inc(s, 1)
            dve.sem_inc(s_hlo, 1)
            dve.sem_inc(s_g, 1)
            dve.sem_inc(s_add, 1)
            dve.wait_ge(s_vec, 32)
            dve.sem_inc(o_l, 16)
            dve.sem_inc(o_so, 32)
            dve.sem_inc(o_m, 16)
            dve.memset(m_col[:, :], 0.0).then_inc(s_mc, 1)
            with dve.Fori(0, B) as b:
                def unit_rows_lo(n, r, u):
                    if isinstance(n, int) and n == 0:
                        for t in range(NT):
                            dve.wait_ge(s_xThi, b * NT + (t + 1))
                            dve.tensor_tensor(xT_lo[:, t, :, :], ex[0][:, t % STAGE, :].rearrange("p (c n) -> p c n", c=DC),
                                              xT_hi[:, t, :, :], ALU.subtract).then_inc(s_xTlo, 1)

                def vectors_lo(n, r, u):
                    g = b * E + n
                    dve.wait_ge(s_muhi, g + 1)
                    dve.tensor_scalar(own[r][:, :], inv_n[:, bass.ds(n, 1)], 1.0, None, ALU.mult).then_inc(s_own, 1)
                    dve.tensor_tensor(m_lo[r][:, :, :], m_raw[:, :].rearrange("p (c s) -> p c s", c=DC), m_hi[r][:, :, :], ALU.subtract).then_inc(s_mulo, 1)

                def rows_lo(n, r, u):
                    if isinstance(n, int) and n == 0:
                        for t in range(NT):
                            dve.wait_ge(s_xlhi, b * NT + (t + 1))
                            dve.tensor_tensor(xl_lo[:, t, :], ex[1][:, t % STAGE, :], xl_hi[:, t, :], ALU.subtract).then_inc(s_xllo, 1)

                def maximum(j):
                    def part(n, r, u):
                        g = b * E + n
                        dve.wait_ge(s_cp, g * JG + (j + 1 + JG))
                        dve.tensor_reduce(col[r][:, j:j + 1], logit[:, j, :], AX.X, ALU.max).then_inc(s_max, 1)
                        if j == JG - 1:
                            dve.wait_ge(s_max, g * (JG + 1) + JG)
                            dve.tensor_reduce(col[r][:, 4:5], col[r][:, 0:JG], AX.X, ALU.max).then_inc(s_max, 1)
                            dve.wait_ge(s_max, g * (JG + 1) + JG + 1)
                            dve.tensor_scalar(col[r][:, 5:6], col[r][:, 4:5], -1.0, None, ALU.mult).then_inc(s_neg, 1)
                    return part

                def largest(j):
                    def part(n, r, u):
                        g = b * E + n
                        if isinstance(n, int) and n == 0 and j == 0:
                            dve.wait_ge(s_reset, b + 1)
                        dve.wait_ge(s_most, g * JG + (j + 1))
                        dve.tensor_tensor(most[:, j, :], most[:, j, :], logit[:, j, :], ALU.max).then_inc(s_most, 1)
                    return part

                def total(n, r, u):
                    g = b * E + n
                    dve.wait_ge(s_ex, g * JG + 2 * JG)
                    dve.tensor_reduce(col[r][:, 10:11], col[r][:, 6:10], AX.X, ALU.add).then_inc(s_sum, 1)
                    dve.wait_ge(s_sum, g + 1)
                    dve.reciprocal(col[r][:, 11:12], col[r][:, 10:11]).then_inc(s_rs, 1)

                def split_lo(j):
                    def part(n, r, u):
                        g = b * E + n
                        dve.wait_ge(s_ehi, g * JG + (j + 1))
                        dve.tensor_tensor(eT_lo[j % 2][:, :, :], ps_t[:, j % 2, :].rearrange("p (t s) -> p t s", t=TG),
                                          eT_hi[j % 2][:, :, :], ALU.subtract).then_inc(s_elo, 1)
                    return part

                def slot_in_lo(n, r, u):
                    g = b * E + n
                    dve.wait_ge(s_sThi, g + 1)
                    dve.tensor_tensor(siT_lo[:, :, :], ps_e[:, 0, :].rearrange("p (c s) -> p c s", c=DC),
                                      siT_hi[:, :, :], ALU.subtract).then_inc(s_sTlo, 1)

                def hidden_lo(n, r, u):
                    g = b * E + n
                    dve.wait_ge(s_hhi, g + 1)
                    dve.tensor_tensor(h_lo[:, :], h[:, :], h_hi[:, :], ALU.subtract).then_inc(s_hlo, 1)

                def bias(n, r, u):
                    g = b * E + n
                    dve.wait_ge(s_b2, g * 16 + 16)
                    dve.wait_ge(s_o, g + 2)
                    dve.tensor_tensor(so[:, :], ps_e[:, 0, :], b2_r[:, :], ALU.add).then_inc(s_add, 1)

                def out_lo(n, r, u):
                    g = b * E + n
                    dve.wait_ge(s_ohi, g + 1)
                    dve.tensor_tensor(so_lo[:, :], so[:, :], so_hi[:, :], ALU.subtract).then_inc(s_olo, 1)

                def weights_lo(n, r, u):
                    g = b * E + n
                    dve.wait_ge(s_whi, g * 2 + 2)
                    dve.wait_ge(s_g, g + 1)
                    dve.tensor_scalar(own_b1[:, :], b1_c[:, bass.ds(n, 1)], 1.0, None, ALU.mult).then_inc(s_own, 1)
                    dve.tensor_tensor(w1_lo[:, :, :], w1_raw[:, :].rearrange("p (c h) -> p c h", c=DC), w1_hi[:, :, :], ALU.subtract).then_inc(s_wlo, 1)
                    dve.tensor_tensor(w2_lo[:, :], w2_raw[:, :], w2_hi[:, :], ALU.subtract).then_inc(s_wlo, 1)

                skewed(dve, [(3, slot_in_lo), (1, maximum(0)), (1, largest(0)), (1, maximum(1)), (1, largest(1)), (1, maximum(2)),
                             (3, hidden_lo), (2, split_lo(0)), (1, maximum(3)), (2, split_lo(1)), (3, bias),
                             (1, largest(2)), (2, split_lo(2)), (1, largest(3)), (1, total),
                             (3, out_lo), (2, split_lo(3)), (0, vectors_lo), (0, unit_rows_lo), (1, rows_lo), (2, weights_lo)], E, U)
                for j in range(JG):
                    dve.wait_ge(s_mt, b * JG + (j + 1 + JG))
                    dve.wait_ge(s_mr, b + 1)
                    dve.tensor_reduce(m_col[:, group(j)], ps_l[:, j, :].rearrange("p (t s) -> p t s", t=TG), AX.X, ALU.max).then_inc(s_mc, 1)


def combine(nc, sems, out, d):
    with ExitStack() as ctx:
        al = Names(nc, ctx, sems)
        sem = lambda name: al.sem("p6_" + name)
        U = 4
        ring = lambda name, shape, dt=F32: [al.sbuf(f"p6_{name}{r}", shape, dt) for r in range(U)]
        so = al.sbuf("p6_so", [P, B, 2, E, D], F32R)
        top = al.sbuf("p6_top", [P, B, N])
        one, zero = al.sbuf("p6_one", [P, 1]), al.sbuf("p6_zero", [P, BANK])
        lg = ring("lg", [P, BANK])
        c_hi, c_lo = ring("c_hi", [P, BANK], F32R), ring("c_lo", [P, BANK], F32R)
        acc = al.sbuf("p6_acc", [P, BANK])
        x1, y, res = (al.sbuf(f"p6_{n}", [P, TG, D]) for n in ("x1", "y", "res"))
        inv = al.sbuf("p6_inv", [P, TG])
        n3 = ring("n3", [P, 12])
        ps_o, ps_s = al.psum("p6_ps_o", TG), al.psum("p6_ps_s", 1)
        s_so, s_vec = [[sem(f"so{b}_{k}") for k in range(4)] for b in range(B)], [sem(f"top{b}") for b in range(B)]
        s_lg, s_x1 = [sem(f"lg{r}") for r in range(U)], sem("x1")
        s_one, s_sub, s_ex, s_hi, s_lo, s_acc = (sem(n) for n in ("one", "shifted", "exp", "c_hi", "c_lo", "acc"))
        s_out, s_tot, s_inv0, s_dr, s_y = sem("out"), sem("totals"), sem("inverse"), sem("drained"), sem("y")
        s_bn, s_eps, s_dev, s_inv, s_res = (sem(n) for n in ("bn", "eps", "dev", "inv"  , "res"))
        o_r = sem("stored")
        block = ctx.enter_context(nc.Block())
        STEPS = B * JG * E
        out_d = out.rearrange("b n c -> (b n) c")
        last = lambda part: lambda n, m, G: part(G) if m == E - 1 else None

        def load_slots(eng, b, k):
            for half in range(2):
                eng.dma_start(so[:, b, half, bass.ts(k, E // 4), :].bitcast(F32), d["so"][b, half, :, bass.ts(k, E // 4), :]).then_inc(s_so[b][k], 16)

        def load_top(sp, b):
            sp.dma_start(top[:, b, :], d["top"][b].rearrange("t p -> (t p)").partition_broadcast(P)).then_inc(s_vec[b], 16)

        @block.sync
        def _(sp):
            def later(k):
                def part(n, m, G):
                    if isinstance(n, int) and n == 0:
                        if k == 0:
                            load_top(sp, 1)
                        load_slots(sp, 1, k)
                return part

            def load(n, m, G):
                r = m % U
                sp.wait_ge(s_lo, n + 1)
                sp.wait_ge(s_acc, n + 1)
                sp.dma_start(lg[r][:, :], d["logit"][G // JG * E + m, :, bass.ds(G % JG * BLK, BLK)]).then_inc(s_lg[r], 16)

            def load_x1(n, m, G):
                if m == 0:
                    sp.wait_ge(s_y, G * TG + TG)
                    sp.dma_start(x1[:, :, :], d["x1"][bass.ds(G * BLK, BLK), :].rearrange("(t p) c -> p t c", p=P)).then_inc(s_x1, 16)

            def store(G):
                sp.wait_ge(s_res, G * TG + 2 * TG)
                sp.dma_start(out_d[bass.ds(G * BLK, BLK), :].rearrange("(t p) c -> p t c", p=P), res[:, :, :]).then_inc(o_r, 16)

            load_top(sp, 0)
            skewed(sp, [(0, load), (9, load_x1), (12, last(store))] + [(E + 2 + 4 * k, later(k)) for k in range(3)]
                   + [(2 * E - 1, later(3))], STEPS, E)
            sp.wait_ge(o_r, 16 + 16 * STEPS // E)

        @block.gpsimd
        def _(pool):
            pool.sem_inc(s_acc, U)
            pool.wait_ge(s_one, 2)

            def accumulate(n, m, G):
                r = m % U
                pool.wait_ge(s_ex, n + 1)
                if m == 0:
                    pool.wait_ge(s_tot, G + 1)
                pool.wait_ge(s_acc, n + U)
                pool.tensor_tensor(acc[:, :], zero[:, :] if m == 0 else acc[:, :], lg[r][:, :], ALU.add).then_inc(s_acc, 1)

            skewed(pool, [(0, accumulate)], STEPS, E)

        @block.tensor
        def _(pe):
            pe.sem_inc(s_out, U)
            pe.sem_inc(s_tot, 1)

            def product(n, m, G):
                b, r = G // JG, m % U
                if m % 4 == 0:
                    pe.wait_ge(s_so[0][m // 4], 32)
                    pe.wait_ge(s_so[1][m // 4], b * 32 + 32)
                pe.wait_ge(s_lo, n + 1 + U)
                for t in range(TG):
                    if m == 0:
                        pe.wait_ge(s_dr, G * TG + (t + 1))
                    rhs = [so[:, bass.ds(b, 1), half, m, :].rearrange("p b n -> p (b n)") for half in range(2)]
                    mm = three_passes(pe, ps_o[:, t, :], c_hi[r][:, bass.ts(t, P)], c_lo[r][:, bass.ts(t, P)], rhs[0], rhs[1],
                                      m == 0, m == E - 1)
                mm.then_inc(s_out, 1)

            def totals(G):
                pe.wait_ge(s_acc, G * E + (E + U))
                pe.wait_ge(s_inv0, G + 1)
                for t in range(TG):
                    mm = pe.matmul(ps_s[:, 0, t:t + 1], acc[:, bass.ts(t, P)], one[:, :], start=True, stop=True)
                mm.then_inc(s_tot, 1)

            for k in range(4):
                pe.sem_inc(s_so[1][k], 32)
            pe.wait_ge(s_one, 1)
            skewed(pe, [(0, product), (0, last(totals))], STEPS, E)

        @block.scalar
        def _(act):
            act.sem_inc(s_res, TG)
            for k in range(4):
                load_slots(act, 0, k)

            def exp(n, m, G):
                r = m % U
                act.wait_ge(s_sub, n + 1)
                act.activation(lg[r][:, :], lg[r][:, :], ACT.Exp).then_inc(s_ex, 1)
                act.wait_ge(s_ex, n + 1)
                act.wait_ge(s_out, n + 1)
                act.activation(c_hi[r][:, :], lg[r][:, :], ACT.Copy).then_inc(s_hi, 1)

            def drain(G):
                act.wait_ge(s_out, G * E + (E + U))
                for t in range(TG):
                    act.wait_ge(s_res, G * TG + (t + 1))
                    act.activation(y[:, t, :], ps_o[:, t, :], ACT.Copy).then_inc(s_dr, 1)

            def deviation(t):
                def part(G):
                    act.wait_ge(s_eps, G * TG + (t + 1))
                    act.activation(n3[t][:, 9:10], n3[t][:, 8:9], ACT.Sqrt).then_inc(s_dev, 1)
                return last(part)

            def result(G):
                for t in range(TG):
                    act.wait_ge(s_inv, G * 2 * TG + 2 * (t + 1))
                    act.wait_ge(o_r, G * 16 + 16)
                    act.activation(res[:, t, :], y[:, t, :], ACT.Identity, scale=n3[t][:, 10:11], bias=n3[t][:, 11:12]).then_inc(s_res, 1)

            skewed(act, [(0, exp), (3, last(drain))] + [(8, deviation(t)) for t in range(TG)] + [(9, last(result))], STEPS, E)

        @block.vector
        def _(dve):
            dve.sem_inc(s_lo, U)
            dve.sem_inc(s_y, TG)
            dve.sem_inc(s_dr, TG)
            dve.sem_inc(s_inv0, 1)
            dve.sem_inc(s_vec[1], 16)
            dve.sem_inc(o_r, 16)
            dve.memset(one[:, :], 1.0).then_inc(s_one, 1)
            dve.memset(zero[:, :], 0.0).then_inc(s_one, 1)
            dve.wait_ge(s_vec[0], 16)

            def shift(n, m, G):
                r = m % U
                if m == 0:
                    dve.wait_ge(s_vec[1], G // JG * 16 + 16)
                dve.wait_ge(s_lg[r], G * (16 * E // U) + (m // U * 16 + 16))
                dve.tensor_tensor(lg[r][:, :], lg[r][:, :], top[:, bass.ds(G // JG, 1), bass.ds(G % JG * BLK, BLK)]
                                  .rearrange("p b n -> p (b n)"), ALU.subtract).then_inc(s_sub, 1)

            def split_lo(n, m, G):
                r = m % U
                dve.wait_ge(s_hi, n + 1)
                dve.tensor_tensor(c_lo[r][:, :], lg[r][:, :], c_hi[r][:, :], ALU.subtract).then_inc(s_lo, 1)

            def residual(t):
                def part(G):
                    if t == 0:
                        dve.wait_ge(s_tot, G + 2)
                        dve.reciprocal(inv[:, :], ps_s[:, 0, 0:TG]).then_inc(s_inv0, 1)
                        dve.wait_ge(s_inv0, G + 2)
                        dve.wait_ge(s_x1, G * 16 + 16)
                    dve.wait_ge(s_dr, G * TG + (t + 1 + TG))
                    dve.scalar_tensor_tensor(y[:, t, :], y[:, t, :], inv[:, t:t + 1], x1[:, t, :], ALU.mult, ALU.add).then_inc(s_y, 1)
                return last(part)

            def statistics(t):
                def part(G):
                    small = n3[t]
                    dve.wait_ge(s_y, G * TG + (t + 1 + TG))
                    dve.bn_stats(small[:, 0:6], y[:, t, :]).then_inc(s_bn, 1)
                    dve.wait_ge(s_bn, G * 3 * TG + (3 * t + 1))
                    dve.memset(small[:, 8:9], LN_EPS).then_inc(s_bn, 1)
                    dve.bn_aggr(small[:, 6:8], small[:, 0:6]).then_inc(s_bn, 1)
                    dve.wait_ge(s_bn, G * 3 * TG + (3 * t + 3))
                    dve.tensor_tensor(small[:, 8:9], small[:, 7:8], small[:, 8:9], ALU.add).then_inc(s_eps, 1)
                return last(part)

            def inverse(G):
                for t in range(TG):
                    small = n3[t]
                    dve.wait_ge(s_dev, G * TG + (t + 1))
                    dve.reciprocal(small[:, 10:11], small[:, 9:10]).then_inc(s_inv, 1)
                    dve.wait_ge(s_inv, G * 2 * TG + (2 * t + 1))
                    dve.tensor_scalar(small[:, 11:12], small[:, 6:7], small[:, 10:11], -1.0, ALU.mult, ALU.mult).then_inc(s_inv, 1)

            skewed(dve, [(0, shift), (1, split_lo)] + [(3 + t, residual(t)) for t in range(TG)]
                   + [(4 + t, statistics(t)) for t in range(TG)] + [(8, last(inverse))], STEPS, E)


def layer(nc, x, Wq, Wk, Wv, Wo, bo, gamma, beta, mu, scale, W1, b1_t, W2, b2, out):
    def scratch(name, shape):
        return nc.dram_tensor(name, shape, F32).ap()

    d = {
        "q": scratch("q_t", [B, GROUPS, 2, P, N]),
        "k": scratch("k_t", [B, 2, P, N]),
        "v": scratch("v", [TOK, P]),
        "ctx": scratch("ctx_t", [B, GROUPS, P, N]),
        "x1": scratch("x1", [TOK, D]),
        "xl": scratch("x_ln", [TT_ALL, P, D]),
        "xT": scratch("x_unit_t", [TT_ALL, P, DC, P]),
        "inv": scratch("slot_norm", [P, E]),
        "logit": scratch("logits_t", [B * E, P, N]),
        "top": scratch("largest_logit", [B, NT, P]),
        "so": scratch("slot_out", [B, 2, P, E, D]),
    }
    stages = (
        lambda sems: projections(nc, sems, x, Wq, Wk, Wv, d),
        lambda sems: attention(nc, sems, mu, d),
        lambda sems: post(nc, sems, x, Wo, bo, gamma, beta, scale, d),
        lambda sems: slots(nc, sems, mu, W1, b1_t, W2, b2, d),
        lambda sems: combine(nc, sems, out, d),
    )
    for stage in stages:
        sems = []
        stage(sems)
        nc.clear_and_free_semaphores(sems)
        nc.all_engine_barrier()


_INS = ["L0_attn_x", "L0_attn_Wq", "L0_attn_Wk", "L0_attn_Wv", "L0_attn_Wo", "L0_attn_bo", "L0_ffn_gamma", "L0_ffn_beta",
        "L0_ffn_mu", "L0_ffn_scale", "L0_ffn_W1", "L0_ffn_b1", "L0_ffn_W2", "L0_ffn_b2"]


def kernel(**inputs):
    import concourse.bacc as bacc
    from concourse.bass_utils import run_bass_kernel_spmd

    nc = bacc.Bacc("TRN2", target_bir_lowering=False, num_devices=1)
    arrays, args = {}, []
    for name in _INS:
        a = np.ascontiguousarray(inputs[name].T if name == "L0_ffn_b1" else inputs[name])
        arrays[name + "_dram"] = a
        args.append(nc.dram_tensor(name + "_dram", a.shape, mybir.dt.from_np(a.dtype), kind="ExternalInput").ap())
    out = nc.dram_tensor("out_dram", [B, N, D], F32, kind="ExternalOutput").ap()
    layer(nc, *args, out)
    r = run_bass_kernel_spmd(nc, [arrays], core_ids=[0])
    return r.results[0]["out_dram"]
```
